# Optimizing a Trainium2 kernel written in Bass

```python
import numpy as np
import jax
import jax.numpy as jnp

def _softmax(x, axis=-1):
    return jax.nn.softmax(x, axis=axis)

def _gelu(x):
    return jax.nn.gelu(x, approximate=True)

def _silu(x):
    return jax.nn.silu(x)

def _sigmoid(x):
    return jax.nn.sigmoid(x)

def _layernorm(x, axis=-1, eps=1e-05):
    m = jnp.mean(x, axis=axis, keepdims=True)
    v = jnp.var(x, axis=axis, keepdims=True)
    return (x - m) / jnp.sqrt(v + eps)

def _scatter_add(tgt, idx, src, axis=0):
    return tgt.at[idx].add(src)

def _segment_sum(src, seg, n):
    return jax.ops.segment_sum(src, seg, n)
kernel_name = 'mk_macaron_d1_jaxref_r8_83ef56'

def setup_inputs(seed: int=0):
    np.random.seed(seed)
    _w = jnp.asarray

    def _L0_attn_setup():
        import jax, jax.numpy as jnp
        import numpy as np
        LN_EPS = 1e-05
        NUM_HEAD = 16
        key = jax.random.key(seed)
        ks = jax.random.split(key, 10)
        B, S, E = (2, 256, 128)
        sc = 0.02
        return {'x': jax.random.normal(ks[0], (B, S, E), jnp.float32), 'wq': jax.random.normal(ks[1], (E, E), jnp.float32) * sc, 'bq': jax.random.normal(ks[2], (E,), jnp.float32) * sc, 'wk': jax.random.normal(ks[3], (E, E), jnp.float32) * sc, 'bk': jax.random.normal(ks[4], (E,), jnp.float32) * sc, 'wv': jax.random.normal(ks[5], (E, E), jnp.float32) * sc, 'bv': jax.random.normal(ks[6], (E,), jnp.float32) * sc, 'wo': jax.random.normal(ks[7], (E, E), jnp.float32) * sc, 'bo': jax.random.normal(ks[8], (E,), jnp.float32) * sc, 'gamma': jnp.ones((E,), jnp.float32), 'beta': jnp.zeros((E,), jnp.float32)}
    _L0_attn_in = _L0_attn_setup()

    def _L0_ffn_setup():
        import jax, jax.numpy as jnp
        import numpy as np
        B, S, D = (1, 256, 128)
        E, K, F = (64, 8, 96)
        SF = 96
        C = 64
        ROUTED_SCALE = 1.0

        def _moe_forward(x, router_w, w_gate, w_up, w_down, ws_gate_up, ws_down):
            T = x.shape[0]
            logits = x.astype(jnp.float32) @ router_w.T
            probs = jax.nn.softmax(logits, axis=-1)
            topk_w, topk_ids = jax.lax.top_k(probs, K)
            topk_w = topk_w / jnp.sum(topk_w, axis=-1, keepdims=True)
            topk_w = topk_w.astype(x.dtype)
            N = T * K
            flat_e = topk_ids.reshape(-1)
            flat_w = topk_w.reshape(-1)
            tok = jnp.arange(N) // K
            onehot = flat_e[:, None] == jnp.arange(E)[None, :]
            pos = jnp.cumsum(onehot, axis=0)[jnp.arange(N), flat_e] - 1
            valid = pos < C
            idx = jnp.where(valid, flat_e * C + pos, E * C)
            x_buf = jnp.zeros((E * C + 1, x.shape[1]), x.dtype).at[idx].set(x[tok])
            xb = x_buf[:E * C].reshape(E, C, -1)
            g = jnp.einsum('ecd,edf->ecf', xb, w_gate)
            u = jnp.einsum('ecd,edf->ecf', xb, w_up)
            h = jax.nn.silu(g) * u
            y = jnp.einsum('ecf,efd->ecd', h, w_down).reshape(E * C, -1)
            safe = jnp.where(valid, idx, 0)
            contrib = y[safe] * (flat_w * valid.astype(flat_w.dtype))[:, None]
            routed = jax.ops.segment_sum(contrib, tok, num_segments=T)
            routed = routed * ROUTED_SCALE
            gu = x @ ws_gate_up
            sg, su = (gu[:, :SF], gu[:, SF:])
            shared = jax.nn.silu(sg) * su @ ws_down
            return routed + shared
        key = jax.random.key(seed)
        ks = jax.random.split(key, 7)
        w = 0.02
        return {'hidden_states': jax.random.normal(ks[0], (B, S, D), jnp.float32), 'router_w': jax.random.normal(ks[1], (E, D), jnp.float32) * w, 'w_gate': jax.random.normal(ks[2], (E, D, F), jnp.float32) * w, 'w_up': jax.random.normal(ks[3], (E, D, F), jnp.float32) * w, 'w_down': jax.random.normal(ks[4], (E, F, D), jnp.float32) * w, 'ws_gate_up': jax.random.normal(ks[5], (D, 2 * SF), jnp.float32) * w, 'ws_down': jax.random.normal(ks[6], (SF, D), jnp.float32) * w}
    _L0_ffn_in = _L0_ffn_setup()
    _d = {'L0_attn_x': _L0_attn_in['x'], 'L0_attn_wq': _L0_attn_in['wq'], 'L0_attn_bq': _L0_attn_in['bq'], 'L0_attn_wk': _L0_attn_in['wk'], 'L0_attn_bk': _L0_attn_in['bk'], 'L0_attn_wv': _L0_attn_in['wv'], 'L0_attn_bv': _L0_attn_in['bv'], 'L0_attn_wo': _L0_attn_in['wo'], 'L0_attn_bo': _L0_attn_in['bo'], 'L0_attn_gamma': _L0_attn_in['gamma'], 'L0_attn_beta': _L0_attn_in['beta'], 'L0_ffn_router_w': _L0_ffn_in['router_w'], 'L0_ffn_w_gate': _L0_ffn_in['w_gate'], 'L0_ffn_w_up': _L0_ffn_in['w_up'], 'L0_ffn_w_down': _L0_ffn_in['w_down'], 'L0_ffn_ws_gate_up': _L0_ffn_in['ws_gate_up'], 'L0_ffn_ws_down': _L0_ffn_in['ws_down']}
    _x0 = _d['L0_attn_x']
    _d['L0_attn_x'] = jax.random.normal(jax.random.fold_in(jax.random.key(seed), 1), (8, 512, 128), dtype=_x0.dtype)
    del _x0
    return _d

def reference(L0_attn_x, L0_attn_wq, L0_attn_bq, L0_attn_wk, L0_attn_bk, L0_attn_wv, L0_attn_bv, L0_attn_wo, L0_attn_bo, L0_attn_gamma, L0_attn_beta, L0_ffn_router_w, L0_ffn_w_gate, L0_ffn_w_up, L0_ffn_w_down, L0_ffn_ws_gate_up, L0_ffn_ws_down):

    def _L0_attn_ref(x, wq, bq, wk, bk, wv, bv, wo, bo, gamma, beta):
        import jax, jax.numpy as jnp
        import numpy as np
        LN_EPS = 1e-05
        NUM_HEAD = 16
        B, S, E = x.shape
        H = NUM_HEAD
        D = E // H
        Q = x @ wq + bq
        K = x @ wk + bk
        V = x @ wv + bv
        Q = Q.reshape(B * H, S, D)
        K = K.reshape(B * H, S, D)
        V = V.reshape(B * H, S, D)
        scores = jnp.einsum('bqd,bkd->bqk', Q, K) / jnp.sqrt(jnp.float32(D))
        attn = jax.nn.softmax(scores, axis=-1)
        ctx = jnp.einsum('bqk,bkd->bqd', attn, V)
        ctx = ctx.reshape(B, S, E)
        out = ctx @ wo + bo
        out = out + x
        mu = jnp.mean(out, axis=-1, keepdims=True)
        var = jnp.var(out, axis=-1, keepdims=True)
        out = (out - mu) * jax.lax.rsqrt(var + LN_EPS) * gamma + beta
        return out

    def _L0_ffn_ref(hidden_states, router_w, w_gate, w_up, w_down, ws_gate_up, ws_down):
        import jax, jax.numpy as jnp
        import numpy as np
        B, S, D = (1, 256, 128)
        E, K, F = (64, 8, 96)
        SF = 96
        C = 64
        ROUTED_SCALE = 1.0

        def _moe_forward(x, router_w, w_gate, w_up, w_down, ws_gate_up, ws_down):
            T = x.shape[0]
            logits = x.astype(jnp.float32) @ router_w.T
            probs = jax.nn.softmax(logits, axis=-1)
            topk_w, topk_ids = jax.lax.top_k(probs, K)
            topk_w = topk_w / jnp.sum(topk_w, axis=-1, keepdims=True)
            topk_w = topk_w.astype(x.dtype)
            N = T * K
            flat_e = topk_ids.reshape(-1)
            flat_w = topk_w.reshape(-1)
            tok = jnp.arange(N) // K
            onehot = flat_e[:, None] == jnp.arange(E)[None, :]
            pos = jnp.cumsum(onehot, axis=0)[jnp.arange(N), flat_e] - 1
            valid = pos < C
            idx = jnp.where(valid, flat_e * C + pos, E * C)
            x_buf = jnp.zeros((E * C + 1, x.shape[1]), x.dtype).at[idx].set(x[tok])
            xb = x_buf[:E * C].reshape(E, C, -1)
            g = jnp.einsum('ecd,edf->ecf', xb, w_gate)
            u = jnp.einsum('ecd,edf->ecf', xb, w_up)
            h = jax.nn.silu(g) * u
            y = jnp.einsum('ecf,efd->ecd', h, w_down).reshape(E * C, -1)
            safe = jnp.where(valid, idx, 0)
            contrib = y[safe] * (flat_w * valid.astype(flat_w.dtype))[:, None]
            routed = jax.ops.segment_sum(contrib, tok, num_segments=T)
            routed = routed * ROUTED_SCALE
            gu = x @ ws_gate_up
            sg, su = (gu[:, :SF], gu[:, SF:])
            shared = jax.nn.silu(sg) * su @ ws_down
            return routed + shared
        b, s, d = hidden_states.shape
        x = hidden_states.reshape(-1, d)
        out = _moe_forward(x, router_w, w_gate, w_up, w_down, ws_gate_up, ws_down)
        return out.reshape(b, s, d)
    x = L0_attn_x
    x = x + 0.5 * _L0_ffn_ref(_layernorm(x, axis=-1), L0_ffn_router_w, L0_ffn_w_gate, L0_ffn_w_up, L0_ffn_w_down, L0_ffn_ws_gate_up, L0_ffn_ws_down)
    x = x + _L0_attn_ref(_layernorm(x, axis=-1), L0_attn_wq, L0_attn_bq, L0_attn_wk, L0_attn_bk, L0_attn_wv, L0_attn_bv, L0_attn_wo, L0_attn_bo, L0_attn_gamma, L0_attn_beta)
    x = x + 0.5 * _L0_ffn_ref(_layernorm(x, axis=-1), L0_ffn_router_w, L0_ffn_w_gate, L0_ffn_w_up, L0_ffn_w_down, L0_ffn_ws_gate_up, L0_ffn_ws_down)
    return x

_drawn_inputs = setup_inputs


def setup_inputs(seed=0):
    import zlib

    import numpy as np

    out = dict(_drawn_inputs(seed))
    spreads = {'L0_attn_gamma': (1.0, 0.2), 'L0_attn_beta': (0.0, 0.1)}
    factors = {'L0_attn_wq': 8.0,
     'L0_attn_bq': 8.0,
     'L0_attn_wk': 8.0,
     'L0_attn_bk': 8.0,
     'L0_attn_wv': 8.0,
     'L0_attn_bv': 8.0,
     'L0_attn_wo': 8.0,
     'L0_attn_bo': 5.335,
     'L0_ffn_router_w': 8.0,
     'L0_ffn_w_gate': 8.0,
     'L0_ffn_w_up': 8.0,
     'L0_ffn_w_down': 8.0,
     'L0_ffn_ws_gate_up': 8.0,
     'L0_ffn_ws_down': 8.0}
    for name, (base, spread) in spreads.items():
        noise = np.random.default_rng([zlib.crc32(name.encode()), seed]).standard_normal(out[name].shape)
        drawn = base * np.exp(spread * noise) if base else spread * noise
        out[name] = jnp.asarray(drawn.astype(out[name].dtype))
    for name, factor in factors.items():
        out[name] = (out[name] * factor).astype(out[name].dtype)
    return out
```

```python
from contextlib import ExitStack

import concourse.bass as bass
from concourse import mybir

F32 = mybir.dt.float32
BF16 = mybir.dt.bfloat16
U32 = mybir.dt.uint32
ALU = mybir.AluOpType
ACT = mybir.ActivationFunctionType
X = mybir.AxisListType.X
P = 128


def macaron_kernel(nc, x_in, wq, bq, wk, bk, wv, bv, wo, bo, gamma, beta,
                   router_w, w_gate, w_up, w_down, ws_gate_up, ws_down, out):
    B, S, D = x_in.shape
    T = B * S
    NT = T // P
    E, _, F = w_gate.shape
    K8, C = 8, 64
    NP2 = E // 2
    GT = 4
    NG = NT // GT
    NACC = 4
    ACC = T + C
    XW = D + E
    H, HD = 16, 8
    HS = S // H
    NH = P // HS
    TERMS = [(0, 0), (0, 1), (1, 0), (1, 1), (0, 2), (2, 0)]
    NR = len(TERMS) * HD
    KR = NR + 2
    SCALE = float(HD) ** -0.5
    LN_EPS = 1e-5
    NBUF = 4
    NPB = 8
    AW = 19072
    assert NH * HS == P and C * 2 == P and T % (P * GT) == 0

    x_rows = x_in.rearrange("b s d -> (b s) d")
    out_rows = out.rearrange("b s d -> (b s) d")
    xw_dram = [nc.dram_tensor(f"dispatch_rows{p}", [T, XW], F32, kind="Internal").ap() for p in range(2)]
    acc_dram = [nc.dram_tensor(f"routed_sums{p}", [NACC * ACC, D], F32, kind="Internal").ap() for p in range(2)]

    with ExitStack() as ctx:
        def sb(name, shape, dt=F32):
            return ctx.enter_context(nc.sbuf_tensor(name, shape, dt))

        def sem(name):
            return ctx.enter_context(nc.semaphore(name))

        def wait(eng, s, value):
            if isinstance(s, Event):
                s, value = s.sem, value + s.base
            if isinstance(value, int) and value <= 0:
                return
            eng.wait_ge(s, value)

        def wait_apart(eng, *waits):
            ready = []
            for s, value in waits:
                if isinstance(s, Event):
                    s, value = s.sem, value + s.base
                if not isinstance(value, int):
                    count = eng.alloc_register()
                    eng.reg_mov(count, value)
                    value = count
                ready.append((s, value))
            eng.wait_ge(s_cst, 1)
            for s, value in ready:
                eng.wait_ge(s, value)
                if not isinstance(value, int):
                    eng.free_register(value)

        x_sb = sb("x_sb", [P, NT, D])
        z_sb = sb("z_sb", [P, NT * D])
        xT_all = z_sb[:]
        wg_sb = sb("wg_sb", [P, E, F])
        wu_sb = sb("wu_sb", [P, E, F])
        wd_sb = sb("wd_sb", [F, E, D])
        wsgu_sb = sb("wsgu_sb", [P, 2 * F])
        wsd_sb = sb("wsd_sb", [F, D])
        rw_sb = sb("rw_sb", [E, D])
        rwT = sb("rwT", [P, E])
        ident = sb("ident", [P, P])
        identb = sb("identb", [P, P], BF16)
        zeros = sb("zeros", [P, 10 * D])
        keyt = sb("keyt", [P, NT])
        slot_c = sb("slot_c", [P, 1])
        acc_off = sb("acc_off", [P, NP2])
        stats = sb("stats", [P, NT, 6])
        mv = sb("mv", [P, NT, 2])
        rstd = sb("rstd", [P, NT])
        xw_sb = sb("xw_sb", [P, 2, GT, XW])
        arena = sb("arena", [P, AW])

        used = [0]

        def carve(words, start=None):
            if start is not None:
                used[0] = start
            a = used[0]
            used[0] += words
            assert used[0] <= AW, used[0]
            return arena[:, a:a + words]

        xT_r = [carve(GT * P) for _ in range(2)]
        d_r = [carve(GT * E) for _ in range(2)]
        e_r = [carve(GT * E) for _ in range(2)]
        top_r = [carve(GT * K8) for _ in range(2)]
        m_r = [carve(GT) for _ in range(2)]
        den_r = [carve(GT) for _ in range(2)]
        key = carve(NT * E)
        KT = carve(NT * E)
        cand = carve(C)
        merged = carve(2 * C)
        slots = carve(C)
        kc = carve(NP2)
        tokf = carve(NP2)
        emp = carve(NP2)
        gidx = carve(NP2).bitcast(U32)
        sidx = carve(NP2).bitcast(U32)
        NGB = 8
        gat = [carve(XW) for _ in range(NGB)]
        gT = [carve(2 * P) for _ in range(2)]
        sil = [carve(4 * C) for _ in range(2)]
        hid = [carve(4 * C) for _ in range(2)]
        NYB = 4
        y_r = [carve(D) for _ in range(NYB)]
        acc_r = [carve(GT * D) for _ in range(2 * NACC)]
        shs = [xT_r[0], xT_r[1]]
        shh = [carve(GT * P) for _ in range(2)]

        QC = H * P
        q_st = [carve(QC // 2, 0 if i == 0 else None).bitcast(BF16)[0:KR, :] for i in range(NBUF)]
        k_st_raw = [carve(QC // 2).bitcast(BF16) for i in range(NBUF)]
        k_st = [t[0:KR, :] for t in k_st_raw]
        p_r = [carve(H * HS) for _ in range(NPB)]
        v_all = carve(NBUF * NH * 4 * 32)
        v_r = [v_all[:, i * NH * 128:(i + 1) * NH * 128].rearrange("p (g k c) -> p g k c", g=NH, k=4) for i in range(NBUF)]
        xn_r = [carve(P) for _ in range(2)]
        xTt_r = [carve(P) for _ in range(2)]
        qk_r = [carve(2 * P) for _ in range(2)]
        res_r = [carve(2 * P) for _ in range(2)]
        part_r = [[carve(P).bitcast(BF16) for _ in range(3)] for _ in range(2)]
        ctx_r = [carve(H * HS) for _ in range(2)]
        num_r = [carve(P) for _ in range(2)]
        den2_r = [carve(P) for _ in range(2)]
        cT_r = [carve(P) for _ in range(2)]
        mx_r = [carve(NH * 4) for _ in range(2)]
        mhl_r = [carve(NH * 4).bitcast(BF16) for _ in range(2)]
        mT_r = [carve(2 * P).bitcast(BF16)[0:8, :] for _ in range(2)]

        def heads(stack, rows, g):
            return stack[rows, :].rearrange("r (c g) -> r c g", g=NH)[:, :, g]

        wqk_sb = sb("wqk_sb", [P, 2 * D])
        wv_sb = sb("wv_sb", [P, D])
        wo_sb = sb("wo_sb", [P, D])
        bqk_sb = sb("bqk_sb", [P, 2])
        bv_sb = sb("bv_sb", [P, 32])
        bo_sb = sb("bo_sb", [P, D])
        gamma_sb = sb("gamma_sb", [P, D])
        beta_sb = sb("beta_sb", [P, D])
        statz = sb("statz", [P, NT, 6])
        mvz = sb("mvz", [P, NT, 2])
        rstdz = sb("rstdz", [P, NT])

        psum = ctx.enter_context(nc.psum_tensor("psum", [P, 8 * 512], F32))
        bank = [psum[:, i * 512:(i + 1) * 512] for i in range(8)]

        s_ld = sem("s_ld")
        s_x = sem("x_loaded")
        s_wr = sem("router_loaded")
        s_wsh = sem("shared_loaded")
        s_wexp = sem("experts_loaded")
        s_cst = sem("constants_ready")
        s_cst1 = sem("constants_step")
        s_zero = sem("zeros_ready")
        s_rwp = sem("router_transposed")
        s_rws = sem("router_copied")
        s_acc0 = [sem(f"sums_zeroed{p}") for p in range(2)]
        s_xfin = [sem(f"x_after_ffn{p}") for p in range(2)]
        s_out = sem("out_stored")

        totals = dict(stats_done=NT, var_ready=NT, eps_added=1, std_ready=1, rstd_ready=1,
                      xn_ready=NG, xT_in_psum=NG, xT_copied=2 * NG, logits_in_psum=NG, row_max=NG, shifted_logits=NT,
                      top8_found=NT, top8_marked=NT, keys_ready=NT, exp_ready=NG, masked_exp=NG, exp_sum=NG,
                      exp_recip=NG, weights_ready=NG, keys_transposed=4, keys_copied=4, list_step=38,
                      slots_transposed=1, indices_ready=1, shared_up_in_psum=NG, shared_silu=NG, shared_hidden=NG,
                      shared_out_in_psum=NG, shared_added=NG, slotsT_in_psum=NP2 // 2, slotsT_copied=NP2 // 2,
                      gate_up_in_psum=NP2 // 2, silu_ready=NP2 // 2, hidden_ready=NP2 // 2, y_in_psum=NP2 // 2,
                      y_weighted=2 * NP2, sums_step=(NACC - 1) * NG, sums_added=NG)
        for i in range(2):
            totals[f"rows_stored{i}"] = 16 * NG // 2
            totals[f"scattered{i}"] = 16 * NP2 // 2
            totals[f"sums_loaded{i}"] = 16 * NACC * NG // 2
        for i in range(NGB):
            totals[f"gathered{i}"] = 16 * NP2 // NGB
        ffn_sems = {name: sem(name) for name in totals}

        class Event:

            def __init__(self, name, p):
                self.sem, self.base = ffn_sems[name], p * totals[name]

        class Ffn:

            def __init__(self, p):
                n = lambda s: Event(s, p)
                self.p = p
                self.stat, self.aggr, self.sd, self.rs = n("stats_done"), n("var_ready"), n("std_ready"), n("rstd_ready")
                self.ve = n("eps_added")
                self.xn, self.xtp, self.xts = n("xn_ready"), n("xT_in_psum"), n("xT_copied")
                self.lg, self.mx, self.d = n("logits_in_psum"), n("row_max"), n("shifted_logits")
                self.top, self.rep, self.key = n("top8_found"), n("top8_marked"), n("keys_ready")
                self.ex, self.es, self.den = n("exp_ready"), n("masked_exp"), n("exp_sum")
                self.rden, self.w = n("exp_recip"), n("weights_ready")
                self.xw = [n(f"rows_stored{i}") for i in range(2)]
                self.ktp, self.kts = n("keys_transposed"), n("keys_copied")
                self.rnd = n("list_step")
                self.slp = n("slots_transposed")
                self.idx = n("indices_ready")
                self.shp, self.shs, self.shh = n("shared_up_in_psum"), n("shared_silu"), n("shared_hidden")
                self.sho, self.shx = n("shared_out_in_psum"), n("shared_added")
                self.gat = [n(f"gathered{i}") for i in range(NGB)]
                self.gtp, self.gts = n("slotsT_in_psum"), n("slotsT_copied")
                self.gu, self.sil, self.hid = n("gate_up_in_psum"), n("silu_ready"), n("hidden_ready")
                self.y, self.ys = n("y_in_psum"), n("y_weighted")
                self.sca = [n(f"scattered{i}") for i in range(2)]
                self.accl = [n(f"sums_loaded{i}") for i in range(2)]
                self.add, self.acca = n("sums_step"), n("sums_added")

        ffns = [Ffn(0), Ffn(1)]
        s_watt = sem("att_weights_loaded")
        s_wqk = sem("wqk_permuted")
        s_vini = sem("v_ring_filled")
        s_vst = sem("v_ring_step")
        a_stat, a_aggr, a_ve, a_sd, a_rs = sem("a_stats"), sem("a_var"), sem("a_eps"), sem("a_std"), sem("a_rstd")
        a_xn = sem("a_xn_ready")
        a_zb = sem("a_residual_ready")
        a_xb = sem("a_x_plus_beta")
        a_use = sem("a_misc_written")
        a_read = sem("a_misc_read")
        a_part1, a_res1, a_part2, a_parts = sem("a_part1"), sem("a_rest1"), sem("a_part2"), sem("a_parts_ready")
        a_stk = [sem(f"a_stack_loaded{i}") for i in range(NBUF)]
        a_mrow = [sem(f"a_max_rows_loaded{i}") for i in range(NBUF)]
        a_S, a_mx = sem("a_scores_in_psum"), sem("a_max_ready")
        a_hi, a_hl = sem("a_max_high"), sem("a_max_split")
        a_ST, a_P, a_PV = sem("a_scoresT_in_psum"), sem("a_exp_ready"), sem("a_pv_done")
        a_cx = sem("a_ctx_copied")
        a_cd = [sem(f"a_ctx_moved{i}") for i in range(2)]
        a_rc, a_ct = sem("a_recip"), sem("a_ctxT_ready")
        a_zs, a_za = sem("a_z_stats"), sem("a_z_var")
        a_zve, a_zsd, a_zrs = sem("a_z_eps"), sem("a_z_std"), sem("a_z_rstd")
        a_fin1, a_fin = sem("a_final_scaled"), sem("a_final_added")

        def use(kind, t):
            if isinstance(t, int):
                special = {("m", 0): 6, ("m", 1): 10, ("m", NT - 1): 156}
                if kind in "xqv" and t < 4:
                    return [0, 3, 7, 11][t] + "xqv".index(kind)
                if kind == "o" and t > 27:
                    return [155, 157, 158, 159][t - 28]
                if (kind, t) in special:
                    return special[kind, t]
            return {"m": 5 * t + 4, "o": 5 * t + 18}[kind] if kind in "mo" else 5 * t - 5 + "xqv".index(kind)

        def lap(n, r, ring, per):
            return n * (per // ring) + (per - r * (per // ring))

        block = ctx.enter_context(nc.Block())

        @block.sync
        def _(sp):
            sp.dma_start(x_sb[:], x_rows.rearrange("(i p) d -> p i d", p=P)).then_inc(s_x, 16)
            sp.dma_start(rw_sb[:], router_w).then_inc(s_wr, 16)
            sp.dma_start(wsgu_sb[:], ws_gate_up).then_inc(s_wsh, 16)
            sp.dma_start(wsd_sb[:], ws_down).then_inc(s_wsh, 16)
            for w, t in ((w_gate, wg_sb), (w_up, wu_sb), (w_down, wd_sb)):
                sp.dma_start(t[:], w.rearrange("e k n -> k e n")).then_inc(s_wexp, 16)
            sp.dma_start(wv_sb[:], wv).then_inc(s_watt, 16)
            sp.dma_start(wo_sb[:], wo.rearrange("(j d) n -> d j n", d=HD)).then_inc(s_watt, 16)
            for i, (w, b) in enumerate(((wq, bq), (wk, bk))):
                sp.dma_start(xw_sb[:, 0, i, 0:D], w).then_inc(s_watt, 16)
                sp.dma_start(bqk_sb[:, i:i + 1], b.rearrange("(j d o) -> d j o", d=HD, o=1), allow_slow_non_contiguous=True).then_inc(s_watt, 16)
            for jj in range(4):
                sp.dma_start(bv_sb[jj * 32:(jj + 1) * 32, :].rearrange("p (k d) -> p k d", k=4),
                             bv.rearrange("(o k jj d) -> jj o k d", o=1, k=4, jj=4)[jj].to_broadcast([32, 4, HD]))\
                  .then_inc(s_watt, 16)
            for t, b in ((bo_sb, bo), (gamma_sb, gamma), (beta_sb, beta)):
                sp.dma_start(t[:], b.rearrange("(o c) -> o c", o=1).to_broadcast([P, D])).then_inc(s_watt, 16)
            sp.wait_ge(s_zero, 1)
            for p in range(2):
                z = acc_dram[p].rearrange("(c p r) d -> c p (r d)", p=P, r=10)
                for c in range(z.shape[0]):
                    sp.dma_start(z[c], zeros[:]).then_inc(s_acc0[p], 16)

            def ffn(f):
                rows = xw_dram[f.p].rearrange("(i p) c -> p i c", p=P)

                def store(g, r):
                    wait(sp, f.w, g + 1)
                    sp.dma_start(rows[:, bass.ds(g * GT, GT), :], xw_sb[:, r, :, :]).then_inc(f.xw[r].sem, 16)
                with sp.Fori(0, NG // 2) as i:
                    for r in range(2):
                        store(2 * i + r, r)
                wait(sp, f.sca[0], 16 * (NP2 // 2))
                wait(sp, f.sca[1], 16 * (NP2 // 2))
                accs = acc_dram[f.p].rearrange("(a t) d -> a t d", a=NACC)[:, 0:T, :].rearrange("a (i p) d -> a p i d", p=P)

                def load(g, r):
                    wait(sp, f.acca, g - 1)
                    for a in range(NACC):
                        sp.dma_start(acc_r[r * NACC + a].rearrange("p (i d) -> p i d", i=GT),
                                     accs[a, :, bass.ds(g * GT, GT), :]).then_inc(f.accl[r].sem, 16)
                load(0, 0)
                load(1, 1)
                with sp.Fori(1, NG // 2) as i:
                    for r in range(2):
                        load(2 * i + r, r)

            def attention():
                def max_rows(t, r):
                    sp.wait_ge(a_read, use("m", t) + 1)
                    for hl in range(2):
                        sp.dma_start(q_st[r][NR + hl:NR + hl + 1, :].rearrange("o (q c) -> o q c", q=4),
                                     mT_r[r % 2][hl * 4:hl * 4 + 4, :]).then_inc(a_mrow[r], 16)

                def stack(t, r):
                    multiplied = 16 * (t - 3)
                    if isinstance(t, int):
                        wait(sp, a_ST, multiplied)
                        sp.wait_ge(a_parts, t + 1)
                    else:
                        split = sp.alloc_register()
                        sp.reg_mov(split, t + 1)
                        sp.wait_ge(a_ST, multiplied)
                        sp.wait_ge(a_parts, split)
                        sp.free_register(split)
                    for i, (a, b) in enumerate(TERMS):
                        for st, part, off in ((q_st, a, 0), (k_st, b, P)):
                            rows = slice(i * HD, (i + 1) * HD)
                            sp.dma_start(st[r][rows, :].rearrange("r (j t) -> r j t", j=H),
                                         part_r[r % 2][part][:, off:off + P]).then_inc(a_stk[r], 16)

                def ctx_move(t, r):
                    sp.wait_ge(a_cx, t + 1)
                    wait(sp, a_use, use("o", t - 2) + 1 if not isinstance(t, int) or t >= 2 else 0)
                    for g in range(NH):
                        for k, dst in enumerate((num_r, den2_r)):
                            a = 32 * g + HD * k
                            sp.dma_start(dst[r % 2][:, g * HS:(g + 1) * HS],
                                         ctx_r[r % 2][a:a + HD, :].rearrange("d (j s) -> d j s", j=H))\
                              .then_inc(a_cd[r % 2], 16)

                sp.wait_ge(s_vini, 2)
                stack(0, 0)
                stack(1, 1)
                max_rows(0, 0)
                stack(2, 2)

                def step(n, r, end=NT):
                    if n is not None and not isinstance(n, int) or n + 1 < end:
                        max_rows(n + 1, (r + 1) % NBUF)
                    if not isinstance(n, int) or n >= 1:
                        ctx_move(n - 1, (r - 1) % NBUF)
                    if not isinstance(n, int) or n + 3 < end:
                        stack(n + 3, (r + 3) % NBUF)
                step(0, 0)
                with sp.Fori(0, 7) as i:
                    for r in range(NBUF):
                        step(4 * i + (r + 1), (r + 1) % NBUF)
                for n in (29, 30, 31):
                    step(n, n % NBUF)
                ctx_move(NT - 1, (NT - 1) % NBUF)

            ffn(ffns[0])
            attention()
            ffn(ffns[1])
            wait(sp, ffns[1].acca, NG)
            sp.dma_start(out_rows.rearrange("(i p) d -> p i d", p=P), x_sb[:]).then_inc(s_out, 16)
            sp.wait_ge(s_out, 16)

        @block.gpsimd
        def _(pool):
            pool.memset(zeros[:], 0.0).then_inc(s_zero, 1)
            pool.memset(ident[:], 0.0).then_inc(s_cst1, 1)
            pool.memset(identb[:], 0.0).then_inc(s_cst1, 1)
            pool.wait_ge(s_cst1, 2)
            for t in (ident, identb):
                pool.affine_select(out=t[:], in_=t[:], compare_op=ALU.not_equal, fill=1.0, base=0,
                                   pattern=[[-1, P]], channel_multiplier=1).then_inc(s_cst, 1)
            f32 = dict(allow_small_or_imprecise_dtypes=True)
            pool.iota(keyt[:], pattern=[[-P, NT]], base=T, channel_multiplier=-1, **f32).then_inc(s_cst, 1)
            for half in range(2):
                rows = slice(half * C, (half + 1) * C)
                pool.wait_ge(s_cst, 3 + 2 * half)
                pool.iota(slot_c[rows, :], pattern=[[0, 1]], base=0, channel_multiplier=1, **f32).then_inc(s_cst, 1)
                pool.iota(acc_off[rows, :], pattern=[[0, NP2 // 2], [2 * ACC, 2]], base=half * ACC,
                          channel_multiplier=0, **f32).then_inc(s_cst, 1)

            def ffn(f):
                wait(pool, f.idx, 1)
                for r in range(2):
                    wait(pool, f.xw[r], 16 * (NG // 2))
                pool.wait_ge(s_acc0[f.p], 16 * (NACC * ACC // (P * 10)))

                def gather(k):
                    wait(pool, f.ys, 4 * ((k - NGB) // 2 + 1) if k >= NGB else 0)
                    pool.indirect_dma_start(out=gat[k % NGB], out_offset=None, in_=xw_dram[f.p],
                                            in_offset=bass.IndirectOffsetOnAxis(ap=gidx[:, k:k + 1], axis=0),
                                            ).then_inc(f.gat[k % NGB].sem, 16)

                LEAD = 6
                for k in range(LEAD):
                    gather(k)
                for k in range(NP2):
                    if k + LEAD < NP2:
                        gather(k + LEAD)
                    wait(pool, f.ys, 4 * (k // 2) + 2 * (k % 2) + 2)
                    wait(pool, f.sca[k % 2], 16 * (k // 2))
                    pool.indirect_dma_start(out=acc_dram[f.p], in_=y_r[k % NYB], in_offset=None,
                                            out_offset=bass.IndirectOffsetOnAxis(ap=sidx[:, k:k + 1], axis=0),
                                            compute_op=ALU.add).then_inc(f.sca[k % 2].sem, 16)

            def attention():
                wait(pool, ffns[0].acca, NG)
                pool.memset(v_all, 0.0).then_inc(s_vst, 1)
                pool.wait_ge(s_vst, 1)
                pool.memset(v_all.rearrange("p (a c) -> p a c", c=32)[:, :, HD:2 * HD], 1.0).then_inc(s_vini, 1)
                for i in range(NBUF):
                    ins = pool.memset(k_st_raw[i][:, :], -1.0)
                ins.then_inc(s_vini, 1)
                pool.wait_ge(s_vini, 2)
                pool.wait_ge(s_watt, 16 * 13)

                def prep(t, r):
                    xt = x_sb[:, bass.ds(t, 1), :].rearrange("p a d -> p (a d)")
                    pool.wait_ge(a_xn, t + 1)
                    pool.tensor_tensor(z_sb[:, bass.ds(t * P, P)], xn_r[r % 2], bo_sb[:], ALU.add).then_inc(a_zb, 1)
                    pool.tensor_tensor(xt, xt, beta_sb[:], ALU.add).then_inc(a_xb, 1)
                    p1, p2, p3 = part_r[r % 2]
                    qk, res = qk_r[r % 2], res_r[r % 2]
                    waits = [(a_read, use("q", t) + 1)]
                    if not isinstance(t, int) or t >= 2:
                        waits.append((a_stk[(r - 2) % NBUF], lap(t - 2, (r - 2) % NBUF, NBUF, 16 * 12)))
                    wait_apart(pool, *waits)
                    pool.tensor_copy(p1, qk).then_inc(a_part1, 1)
                    pool.wait_ge(a_part1, t + 1)
                    pool.tensor_tensor(res, qk, p1, ALU.subtract).then_inc(a_res1, 1)
                    wait_apart(pool, (a_res1, t + 1))
                    pool.tensor_copy(p2, res).then_inc(a_part2, 1)
                    pool.wait_ge(a_part2, t + 1)
                    pool.tensor_tensor(p3, res, p2, ALU.subtract).then_inc(a_parts, 1)

                for t in range(4):
                    prep(t, t)
                with pool.Fori(1, NT // NBUF) as i:
                    for r in range(NBUF):
                        prep(NBUF * i + r, r)

            ffn(ffns[0])
            attention()
            ffn(ffns[1])

        @block.vector
        def _(dve):
            def layernorm_stats(f_stat, f_aggr, f_ve, f_sd, f_rs):
                inc = lambda ins, s: ins.then_inc(s.sem if isinstance(s, Event) else s, 1)
                for i in range(NT):
                    inc(dve.bn_stats(stats[:, i, :], x_sb[:, i, :]), f_stat)
                for i in range(NT):
                    wait(dve, f_stat, i + 1)
                    inc(dve.bn_aggr(mv[:, i, :], stats[:, i, :]), f_aggr)
                wait(dve, f_aggr, NT)
                inc(dve.tensor_scalar(rstd[:], mv[:, :, 1], LN_EPS, None, ALU.add), f_ve)
                wait(dve, f_sd, 1)
                inc(dve.reciprocal(rstd[:], rstd[:]), f_rs)
                wait(dve, f_rs, 1)

            def ffn(f):
                layernorm_stats(f.stat, f.aggr, f.ve, f.sd, f.rs)

                def route(g, r):
                    wait(dve, f.xw[r], 16 * ((g - r) // 2) if isinstance(g, int) else 8 * (g - r))
                    xw = xw_sb[:, r, :, :]
                    for j in range(GT):
                        t = g * GT + j
                        ins = dve.tensor_scalar(xw[:, j, 0:D], x_sb[:, bass.ds(t, 1), :].rearrange("p a d -> p (a d)"),
                                                mv[:, bass.ds(t, 1), 0], rstd[:, bass.ds(t, 1)],
                                                ALU.subtract, ALU.mult)
                    ins.then_inc(f.xn.sem, 1)
                    lg = bank[2 + r][:, 0:GT * E].rearrange("p (j e) -> p j e", j=GT)
                    d = d_r[r].rearrange("p (j e) -> p j e", j=GT)
                    e = e_r[r].rearrange("p (j e) -> p j e", j=GT)
                    top = top_r[r].rearrange("p (j e) -> p j e", j=GT)
                    kk = key.rearrange("p (i e) -> p i e", e=E)
                    wait(dve, f.lg, g + 1)
                    dve.tensor_reduce(m_r[r], lg, X, ALU.max).then_inc(f.mx.sem, 1)
                    wait(dve, f.mx, g + 1)
                    for j in range(GT):
                        dve.tensor_scalar(d[:, j, :], lg[:, j, :], m_r[r][:, j:j + 1], -88.0,
                                          ALU.subtract, ALU.max).then_inc(f.d.sem, 1)
                    for j in range(GT):
                        wait_apart(dve, (f.d, g * GT + j + 1))
                        dve.max(top[:, j, :], d[:, j, :]).then_inc(f.top.sem, 1)
                    for j in range(GT):
                        wait_apart(dve, (f.top, g * GT + j + 1), (f.ex, g + 1))
                        dve.match_replace(d[:, j, :], top[:, j, :], d[:, j, :], 1.0).then_inc(f.rep.sem, 1)
                    for j in range(GT):
                        t = g * GT + j
                        wait(dve, f.rep, g * GT + j + 1)
                        dve.tensor_scalar(kk[:, bass.ds(t, 1), :].rearrange("p a e -> p (a e)"), d[:, j, :], 0.5,
                                          keyt[:, bass.ds(t, 1)], ALU.is_gt, ALU.mult).then_inc(f.key.sem, 1)
                    dve.scalar_tensor_tensor(out=e_r[r], in0=d_r[r], scalar=0.5, in1=e_r[r],
                                             op0=ALU.is_gt, op1=ALU.mult).then_inc(f.es.sem, 1)
                    wait(dve, f.es, g + 1)
                    dve.tensor_reduce(den_r[r], e, X, ALU.add).then_inc(f.den.sem, 1)
                    wait(dve, f.den, g + 1)
                    dve.reciprocal(den_r[r], den_r[r]).then_inc(f.rden.sem, 1)
                    wait(dve, f.rden, g + 1)
                    dve.scalar_tensor_tensor(out=xw[:, :, D:XW], in0=e, scalar=0.5,
                                             in1=den_r[r].unsqueeze(2).to_broadcast([P, GT, E]),
                                             op0=ALU.mult, op1=ALU.mult).then_inc(f.w.sem, 1)

                dve.wait_ge(s_cst, 7)
                route(0, 0)
                route(1, 1)
                with dve.Fori(1, NG // 2) as i:
                    for r in range(2):
                        route(2 * i + r, r)

                step = [0]

                def link(ins):
                    step[0] += 1
                    ins.then_inc(f.rnd.sem, 1)
                    wait(dve, f.rnd, step[0])

                def top_list(dst, src):
                    for c in range(0, C, 8):
                        link(dve.max(dst[:, c:c + 8], src))
                        if c + 8 < C:
                            link(dve.match_replace(src, dst[:, c:c + 8], src, 0.0))

                wait(dve, f.kts, 4)
                top_list(cand, KT)
                link(dve.tensor_copy(merged[0:E, 0:C], cand[0:E, :]))
                link(dve.tensor_copy(merged[0:E, C:2 * C], cand[E:2 * E, :]))
                top_list(slots[0:E, :], merged[0:E, :])
                wait(dve, f.slp, 1)
                both = bank[0][0:C, 0:E].rearrange("c (k two) -> c k two", two=2)
                link(dve.tensor_copy(kc[0:C, :], both[:, :, 0]))
                link(dve.tensor_copy(kc[C:P, :], both[:, :, 1]))
                link(dve.tensor_scalar(tokf, kc, -1.0, float(T), ALU.mult, ALU.add))
                link(dve.tensor_scalar(gidx, tokf, float(T - 1), None, ALU.min))
                link(dve.tensor_scalar(emp, kc, 0.0, slot_c[:, 0:1], ALU.is_equal, ALU.mult))
                link(dve.tensor_tensor(emp, emp, acc_off[:], ALU.add))
                dve.tensor_tensor(sidx, tokf, emp, ALU.add).then_inc(f.idx.sem, 1)

                def shared(g, r):
                    wait(dve, f.shs, g + 1)
                    dve.tensor_tensor(shh[r][0:F, :], shs[r][0:F, :], bank[2 + r][0:F, :], ALU.mult).then_inc(f.shh.sem, 1)
                    wait(dve, f.sho, g + 1)
                    xs = x_sb[:, bass.ds(g * GT, GT), :]
                    dve.scalar_tensor_tensor(out=xs, in0=bank[4 + r][:].rearrange("p (i d) -> p i d", i=GT), scalar=0.5,
                                             in1=xs, op0=ALU.mult, op1=ALU.add).then_inc(f.shx.sem, 1)
                with dve.Fori(0, NG // 2) as i:
                    for r in range(2):
                        shared(2 * i + r, r)

                for q in range(NP2 // 2):
                    r = q % 2
                    wait(dve, f.sil, q + 1)
                    dve.tensor_tensor(hid[r][0:F, :], sil[r][0:F, :], bank[2 + r][0:F, 4 * C:8 * C],
                                      ALU.mult).then_inc(f.hid.sem, 1)
                    wait(dve, f.y, q + 1)
                    for j in range(2):
                        k = 2 * q + j
                        wait(dve, f.sca[k % 2], 16 * ((k - NYB) // 2 + 1) if k >= NYB else 0)
                        for half in range(2):
                            rows = slice(half * C, (half + 1) * C)
                            col = D + 2 * k + half
                            dve.tensor_scalar(y_r[k % NYB][rows, :], bank[4 + r][rows, j * D:(j + 1) * D],
                                              gat[k % NGB][rows, col:col + 1], None, ALU.mult).then_inc(f.ys.sem, 1)

                def add(g, r):
                    xs = x_sb[:, bass.ds(g * GT, GT), :]
                    for a in range(NACC):
                        if a == 0:
                            wait(dve, f.accl[r], 16 * NACC * ((g - r) // 2 + 1) if isinstance(g, int)
                                        else 8 * NACC * (g - r) + 16 * NACC)
                        else:
                            wait(dve, f.add, (g * (NACC - 1)) + a)
                        src = acc_r[r * NACC + a].rearrange("p (i d) -> p i d", i=GT)
                        ins = dve.tensor_tensor(xs, xs, src, ALU.add)
                        ins.then_inc((f.add if a < NACC - 1 else f.acca).sem, 1)
                with dve.Fori(0, NG // 2) as i:
                    for r in range(2):
                        add(2 * i + r, r)
                wait(dve, f.acca, NG)

            def attention():
                layernorm_stats(a_stat, a_aggr, a_ve, a_sd, a_rs)
                dve.wait_ge(s_watt, 16 * 13)

                def xn(t, r):
                    if not isinstance(t, int) or t >= 2:
                        dve.wait_ge(a_zb, t - 1)
                        dve.wait_ge(a_use, use("x", t - 2) + 1)
                    dve.tensor_scalar(xn_r[r % 2], x_sb[:, bass.ds(t, 1), :].rearrange("p a d -> p (a d)"),
                                      mv[:, bass.ds(t, 1), 0], rstd[:, bass.ds(t, 1)],
                                      ALU.subtract, ALU.mult).then_inc(a_xn, 1)

                def v_copy(t, r):
                    dve.wait_ge(a_use, use("v", t) + 1)
                    wait(dve, a_PV, 4 * (t - 3))
                    b = bv_sb[:].rearrange("p (k c) -> p k c", k=4).unsqueeze(1).to_broadcast([P, NH, 4, HD])
                    dve.tensor_tensor(v_r[r][:, :, :, 0:HD], bank[7][:, 0:P].rearrange("p (g k c) -> p g k c", g=NH, k=4),
                                      b, ALU.add).then_inc(a_read, 1)

                def row_max(t, r, p):
                    dve.wait_ge(a_S, 8 * t + (p + 1))
                    src = psum[:, (p % 2) * 1024:(p % 2) * 1024 + 1024].rearrange("p (a k) -> p a k", a=2)
                    dve.tensor_reduce(mx_r[r % 2][:, 2 * p:2 * p + 2], src, X, ALU.max).then_inc(a_mx, 1)

                def max_high(t, r):
                    dve.wait_ge(a_mx, 8 * t + 8)
                    hl = mhl_r[r % 2].rearrange("p (g h q) -> p g h q", g=NH, h=2)
                    mx = mx_r[r % 2].rearrange("p (g q) -> p g q", g=NH)
                    dve.tensor_copy(hl[:, :, 0, :], mx).then_inc(a_hi, 1)

                def max_low(t, r):
                    dve.wait_ge(a_hi, t + 1)
                    hl = mhl_r[r % 2].rearrange("p (g h q) -> p g h q", g=NH, h=2)
                    mx = mx_r[r % 2].rearrange("p (g q) -> p g q", g=NH)
                    dve.tensor_tensor(hl[:, :, 1, :], mx, hl[:, :, 0, :], ALU.subtract).then_inc(a_hl, 1)

                def max_copy(t, r):
                    dve.wait_ge(a_use, use("m", t) + 1)
                    if not isinstance(t, int) or t >= 2:
                        dve.wait_ge(a_mrow[(r - 2) % NBUF], lap(t - 2, (r - 2) % NBUF, NBUF, 16 * 2))
                    dve.tensor_copy(mT_r[r % 2].rearrange("m (c g) -> m g c", g=NH),
                                    bank[7][0:8, 0:2 * P].bitcast(BF16).rearrange("m (g c) -> m g c", g=NH))\
                       .then_inc(a_read, 1)

                def ctx_recip(t, r):
                    dve.wait_ge(a_cd[r % 2], lap(t, r % 2, 2, 16 * 8))
                    dve.reciprocal(den2_r[r % 2], den2_r[r % 2]).then_inc(a_rc, 1)

                def ctx_div(t, r):
                    dve.wait_ge(a_rc, t + 1)
                    wait(dve, a_use, use("o", t - 2) + 1 if not isinstance(t, int) or t >= 2 else 0)
                    dve.tensor_tensor(cT_r[r % 2], num_r[r % 2], den2_r[r % 2], ALU.mult).then_inc(a_ct, 1)

                def z_add(t):
                    dve.wait_ge(a_use, use("o", t) + 1)
                    dve.wait_ge(a_zb, t + 1)
                    z = z_sb[:, bass.ds(t * P, P)]
                    dve.tensor_tensor(z, bank[7][:, 0:P], z, ALU.add).then_inc(a_read, 1)

                def z_stats(t):
                    dve.wait_ge(a_read, use("o", t) + 1)
                    dve.bn_stats(statz[:, bass.ds(t, 1), :].rearrange("p a c -> p (a c)"),
                                 z_sb[:, bass.ds(t * P, P)]).then_inc(a_zs, 1)

                xn(0, 0)
                xn(1, 1)
                dve.wait_ge(s_vini, 2)
                v_copy(0, 0)
                for p in range(8):
                    row_max(0, 0, p)
                max_high(0, 0)
                max_low(0, 0)
                xn(2, 2)
                v_copy(1, 1)
                for p in range(8):
                    row_max(1, 1, p)
                    if p == 0:
                        max_copy(0, 0)
                max_high(1, 1)
                max_low(1, 1)
                xn(3, 3)
                v_copy(2, 2)

                def step(n, r, end=NT):
                    mid = not isinstance(n, int)
                    at = lambda k: (r + k) % NBUF
                    for p in range(8):
                        if mid or n + 2 < end:
                            row_max(n + 2, at(2), p)
                        if p == 0 and (mid or n + 1 < end):
                            max_copy(n + 1, at(1))
                        if p == 3 and (mid or n + 4 < end):
                            xn(n + 4, at(4))
                        if p == 4 and (mid or n + 3 < end):
                            v_copy(n + 3, at(3))
                        if p == 5 and (mid or n >= 1):
                            ctx_recip(n - 1, at(-1))
                            ctx_div(n - 1, at(-1))
                        if p == 6 and (mid or n >= 1):
                            z_add(n - 1)
                    if mid or n >= 1:
                        z_stats(n - 1)
                    if mid or n + 2 < end:
                        max_high(n + 2, at(2))
                        max_low(n + 2, at(2))
                step(0, 0)
                with dve.Fori(0, 6) as i:
                    for r in range(NBUF):
                        step(4 * i + (r + 1), (r + 1) % NBUF)
                for n in range(25, 32):
                    step(n, n % NBUF)
                t = NT - 1
                ctx_recip(t, t % NBUF)
                ctx_div(t, t % NBUF)
                z_add(t)
                z_stats(t)
                for t in range(NT):
                    dve.wait_ge(a_zs, t + 1)
                    dve.bn_aggr(mvz[:, t, :], statz[:, t, :]).then_inc(a_za, 1)
                dve.wait_ge(a_za, NT)
                dve.tensor_scalar(rstdz[:], mvz[:, :, 1], LN_EPS, None, ALU.add).then_inc(a_zve, 1)
                dve.wait_ge(a_zsd, 1)
                dve.reciprocal(rstdz[:], rstdz[:]).then_inc(a_zrs, 1)
                dve.wait_ge(a_zrs, 1)
                dve.wait_ge(a_xb, NT)
                for t in range(NT):
                    z = z_sb[:, t * P:(t + 1) * P]
                    dve.scalar_tensor_tensor(out=z, in0=z, scalar=mvz[:, t, 0:1], in1=gamma_sb[:],
                                             op0=ALU.subtract, op1=ALU.mult).then_inc(a_fin1, 1)
                for t in range(NT):
                    z = z_sb[:, t * P:(t + 1) * P]
                    dve.wait_ge(a_fin1, t + 1)
                    dve.scalar_tensor_tensor(out=x_sb[:, t, :], in0=z, scalar=rstdz[:, t:t + 1], in1=x_sb[:, t, :],
                                             op0=ALU.mult, op1=ALU.add).then_inc(a_fin, 1)
                dve.wait_ge(a_fin, NT)

            dve.wait_ge(s_watt, 16 * 13)
            for i in range(2):
                dve.tensor_copy(wqk_sb[:, i * D:(i + 1) * D].rearrange("k (d j) -> k d j", d=HD),
                                xw_sb[:, 0, i, 0:D].rearrange("k (j d) -> k d j", d=HD)).then_inc(s_wqk, 1)
            dve.wait_ge(s_x, 16)
            dve.wait_ge(s_rwp, 1)
            dve.tensor_copy(rwT[:], bank[0][:, 0:E]).then_inc(s_rws, 1)
            ffn(ffns[0])
            attention()
            ffn(ffns[1])

        @block.scalar
        def _(act):
            def ffn(f):
                wait(act, f.ve, 1)
                act.activation(rstd[:], rstd[:], ACT.Sqrt).then_inc(f.sd.sem, 1)

                def route(g, r):
                    wait(act, f.xtp, g + 1)
                    wait(act, f.lg, g - 1)
                    act.activation(xT_r[r], bank[r][:], ACT.Copy).then_inc(f.xts.sem, 1)
                    act.activation(xT_all[:, bass.ds(g * (GT * P), GT * P)], bank[r][:], ACT.Copy).then_inc(f.xts.sem, 1)
                    wait(act, f.d, GT * (g + 1))
                    wait(act, f.w, g - 1)
                    act.activation(e_r[r], d_r[r], ACT.Exp).then_inc(f.ex.sem, 1)
                route(0, 0)
                route(1, 1)
                with act.Fori(1, NG // 2) as i:
                    for r in range(2):
                        route(2 * i + r, r)
                for b in range(4):
                    wait(act, f.ktp, b + 1)
                    act.activation(KT[:, b * 512:(b + 1) * 512], bank[4 + b][:], ACT.Copy).then_inc(f.kts.sem, 1)

                def shared(g, r):
                    wait(act, f.shp, g + 1)
                    wait(act, f.shh, g - 1)
                    act.activation(shs[r][0:F, :], bank[r][0:F, :], ACT.Silu).then_inc(f.shs.sem, 1)
                shared(0, 0)
                shared(1, 1)
                with act.Fori(1, NG // 2) as i:
                    for r in range(2):
                        shared(2 * i + r, r)

                for q in range(NP2 // 2):
                    r = q % 2
                    wait(act, f.gtp, q + 1)
                    wait(act, f.gu, q - 1)
                    act.activation(gT[r], bank[r][:, 0:2 * P], ACT.Copy).then_inc(f.gts.sem, 1)
                    wait(act, f.gu, q + 1)
                    wait(act, f.hid, q - 1)
                    act.activation(sil[r][0:F, :], bank[2 + r][0:F, 0:4 * C], ACT.Silu).then_inc(f.sil.sem, 1)

            def attention():
                act.wait_ge(a_ve, 1)
                act.activation(rstd[:], rstd[:], ACT.Sqrt).then_inc(a_sd, 1)

                def xT_copy(t, r):
                    act.wait_ge(a_use, use("x", t) + 1)
                    act.activation(xTt_r[r % 2], bank[7][:, 0:P], ACT.Copy).then_inc(a_read, 1)

                def qk_copy(t, r):
                    act.wait_ge(a_use, use("q", t) + 1)
                    wait(act, a_parts, t - 1)
                    for i in range(2):
                        ins = act.activation(qk_r[r % 2][:, i * P:(i + 1) * P].rearrange("p (s g) -> p g s", g=NH),
                                             bank[7][:, i * P:(i + 1) * P].rearrange("p (g s) -> p g s", g=NH),
                                             ACT.Identity, bias=bqk_sb[:, i:i + 1])
                    ins.then_inc(a_read, 1)

                def ctx_copy(t, r):
                    act.wait_ge(a_PV, 4 * t + 4)
                    if not isinstance(t, int) or t >= 2:
                        act.wait_ge(a_cd[r % 2], lap(t - 2, r % 2, 2, 16 * 8))
                    act.activation(ctx_r[r % 2], bank[6][:, :], ACT.Copy).then_inc(a_cx, 1)

                def step(n, r, end=NT):
                    mid = not isinstance(n, int)
                    for tau in range(16):
                        kt, g = tau // 4, tau % 4
                        act.wait_ge(a_ST, 16 * n + (tau + 1))
                        if g == 0:
                            wait(act, a_PV, 4 * n + (kt - 1))
                        act.activation(p_r[tau % NPB], bank[4 + tau % 2][:, :], ACT.Exp, scale=SCALE).then_inc(a_P, 1)
                        if tau == 4 and (mid or n + 3 < end):
                            xT_copy(n + 3, (r + 3) % NBUF)
                        if tau == 5 and (mid or n >= 1):
                            ctx_copy(n - 1, (r - 1) % NBUF)
                        if tau == 7 and (mid or n + 3 < end):
                            qk_copy(n + 3, (r + 3) % NBUF)
                for t in range(3):
                    xT_copy(t, t)
                    qk_copy(t, t)
                step(0, 0)
                with act.Fori(0, 7) as i:
                    for r in range(NBUF):
                        step(4 * i + (r + 1), (r + 1) % NBUF)
                for n in (29, 30, 31):
                    step(n, n % NBUF)
                ctx_copy(NT - 1, (NT - 1) % NBUF)
                act.wait_ge(a_zve, 1)
                act.activation(rstdz[:], rstdz[:], ACT.Sqrt).then_inc(a_zsd, 1)

            ffn(ffns[0])
            attention()
            ffn(ffns[1])

        @block.tensor
        def _(pe):
            def ffn(f):
                def route(g, r):
                    wait(pe, f.xn, g + 1)
                    wait(pe, f.xts, 2 * (g - 1))
                    for j in range(GT):
                        ins = pe.transpose(bank[r][:, j * P:(j + 1) * P], xw_sb[:, r, j, 0:D], ident[:])
                    ins.then_inc(f.xtp.sem, 1)
                    wait(pe, f.xts, 2 * g + 1)
                    wait(pe, f.d, GT * (g - 1))
                    for j in range(GT):
                        ins = pe.matmul(bank[2 + r][:, j * E:(j + 1) * E], xT_r[r][:, j * P:(j + 1) * P], rwT[:],
                                        start=True, stop=True)
                    ins.then_inc(f.lg.sem, 1)
                route(0, 0)
                route(1, 1)
                with pe.Fori(1, NG // 2) as i:
                    for r in range(2):
                        route(2 * i + r, r)

                wait(pe, f.key, NT)
                for u in range(NT // 2):
                    ins = pe.transpose(bank[4 + u // 4][:, (u % 4) * P:(u % 4 + 1) * P], key[:, u * P:(u + 1) * P], ident[:])
                    if u % 4 == 3:
                        ins.then_inc(f.ktp.sem, 1)
                pe.wait_ge(s_wsh, 32)

                def up(g, r):
                    wait(pe, f.shh, g - 1)
                    pe.matmul(bank[r][0:F, :], wsgu_sb[:, 0:F], xT_all[:, bass.ds(g * (GT * P), GT * P)],
                              start=True, stop=True)
                    pe.matmul(bank[2 + r][0:F, :], wsgu_sb[:, F:2 * F], xT_all[:, bass.ds(g * (GT * P), GT * P)],
                              start=True, stop=True).then_inc(f.shp.sem, 1)

                def down(g, r):
                    wait(pe, f.shh, g + 1)
                    wait(pe, f.shx, g - 1)
                    for j in range(GT):
                        ins = pe.matmul(bank[4 + r][:, j * D:(j + 1) * D], shh[r][0:F, j * P:(j + 1) * P], wsd_sb[:],
                                        start=True, stop=True)
                    ins.then_inc(f.sho.sem, 1)

                wait(pe, f.xts, 2 * NG)
                wait(pe, f.kts, 4)
                up(0, 0)
                wait(pe, f.rnd, 32)
                wait(pe, f.shs, 1)
                pe.transpose(bank[0][0:C, 0:E], slots[0:E, :], ident[0:E, 0:E]).then_inc(f.slp.sem, 1)
                up(1, 1)
                down(0, 0)
                wait(pe, f.idx, 1)
                with pe.Fori(1, NG // 2) as i:
                    up(2 * i, 0)
                    down(2 * i - 1, 1)
                    up(2 * i + 1, 1)
                    down(2 * i, 0)
                down(NG - 1, 1)

                pe.wait_ge(s_wexp, 48)

                def slots_t(q):
                    r = q % 2
                    wait(pe, f.gts, q - 1)
                    for j in range(2):
                        k = 2 * q + j
                        wait(pe, f.gat[k % NGB], 16 * (k // NGB + 1))
                        ins = pe.transpose(bank[r][:, j * P:(j + 1) * P], gat[k % NGB][:, 0:D], ident[:])
                    ins.then_inc(f.gtp.sem, 1)

                def down_e(q):
                    r = q % 2
                    wait(pe, f.hid, q + 1)
                    wait(pe, f.ys, 4 * (q - 1))
                    for j in range(2):
                        for half in range(2):
                            e = 4 * q + 2 * j + half
                            rows = slice(half * C, (half + 1) * C)
                            ins = pe.matmul(bank[4 + r][rows, j * D:(j + 1) * D],
                                            hid[r][0:F, (2 * j + half) * C:(2 * j + half + 1) * C], wd_sb[:, e, :],
                                            start=True, stop=True)
                    ins.then_inc(f.y.sem, 1)

                wait(pe, f.shs, NG)
                wait(pe, f.shx, NG)
                slots_t(0)
                for q in range(NP2 // 2):
                    r = q % 2
                    wait(pe, f.gts, q + 1)
                    wait(pe, f.hid, q - 1)
                    for w, off in ((wg_sb, 0), (wu_sb, 4 * C)):
                        for m in range(4):
                            ins = pe.matmul(bank[2 + r][0:F, off + m * C:off + (m + 1) * C], w[:, 4 * q + m, :],
                                            gT[r][:, m * C:(m + 1) * C], start=True, stop=True)
                    ins.then_inc(f.gu.sem, 1)
                    if q + 1 < NP2 // 2:
                        slots_t(q + 1)
                    if q:
                        down_e(q - 1)
                down_e(NP2 // 2 - 1)

            pe.wait_ge(s_cst, 2)
            pe.wait_ge(s_wr, 16)
            pe.transpose(bank[0][:, 0:E], rw_sb[:], ident[0:E, 0:E]).then_inc(s_rwp, 1)
            pe.wait_ge(s_rws, 1)
            def attention():
                def misc(kind, t):
                    i = use(kind, t)
                    wait(pe, a_read, i)

                def xT(t, r):
                    pe.wait_ge(a_xn, t + 1)
                    misc("x", t)
                    pe.transpose(bank[7][:, 0:P], xn_r[r % 2], ident[:]).then_inc(a_use, 1)

                def qk(t, r):
                    misc("q", t)
                    for i in range(2):
                        ins = pe.matmul(bank[7][:, i * P:(i + 1) * P], wqk_sb[:, i * D:(i + 1) * D], xTt_r[r % 2],
                                        start=True, stop=True)
                    ins.then_inc(a_use, 1)

                def v(t, r):
                    misc("v", t)
                    for g in range(NH):
                        for jj in range(4):
                            ins = pe.matmul(bank[7][jj * 32:(jj + 1) * 32, g * 32:(g + 1) * 32],
                                            xTt_r[r % 2][:, g * HS:(g + 1) * HS],
                                            wv_sb[:].rearrange("e (k jj d) -> e jj k d", k=4, jj=4)[:, jj, :, :],
                                            start=True, stop=True, tile_position=(0, jj * 32))
                    ins.then_inc(a_use, 1)

                def maxT(t, r):
                    pe.wait_ge(a_hl, t + 1)
                    misc("m", t)
                    for g in range(NH):
                        ins = pe.transpose(bank[7][0:8, g * P // 2:(g + 1) * P // 2].bitcast(BF16),
                                           mhl_r[r % 2][:, 8 * g:8 * g + 8], identb[:])
                    ins.then_inc(a_use, 1)

                def proj(t, r):
                    pe.wait_ge(a_ct, t + 1)
                    misc("o", t)
                    pe.matmul(bank[7][:, 0:D], cT_r[r % 2], wo_sb[:], start=True, stop=True).then_inc(a_use, 1)

                def scores(t, r, tau):
                    g, qt = tau // 4, tau % 4
                    if tau == 0:
                        pe.wait_ge(a_stk[r], lap(t, r, NBUF, 16 * 12))
                    if tau % 2 == 0:
                        wait(pe, a_mx, 8 * t + (tau // 2 - 1))
                    rows = slice(0, NR)
                    ins = pe.matmul(bank[tau % 4][:, :], heads(q_st[r], rows, g)[:, qt * P:(qt + 1) * P],
                                    heads(k_st[r], rows, g), start=True, stop=True)
                    if tau % 2:
                        ins.then_inc(a_S, 1)

                def scores_t(t, r, tau):
                    kt, g = tau // 4, tau % 4
                    if tau == 0:
                        pe.wait_ge(a_mrow[r], lap(t, r, NBUF, 16 * 2))
                    wait(pe, a_P, 16 * t + (tau - 1))
                    rows = slice(0, KR)
                    keys = heads(k_st[r], rows, g)[:, kt * P:(kt + 1) * P]
                    pe.matmul(bank[4 + tau % 2][:, :], keys, heads(q_st[r], rows, g), start=True, stop=True)\
                      .then_inc(a_ST, 1)

                def pv(t, r, kt):
                    pe.wait_ge(a_P, 16 * t + (4 * kt + 4))
                    if kt == 0:
                        wait(pe, a_cx, t)
                        pe.wait_ge(a_read, use("v", t) + 1)
                    for g in range(NH):
                        ins = pe.matmul(bank[6][32 * g:32 * g + 32, :], v_r[r][:, g, kt, :], p_r[(4 * kt + g) % NPB],
                                        start=(kt == 0), stop=(kt == 3), tile_position=(0, 32 * g))
                    ins.then_inc(a_PV, 1)

                def step(n, r, end=NT):
                    mid = not isinstance(n, int)
                    at = lambda k: (r + k) % NBUF
                    for tau in range(16):
                        if tau == 1 and (mid or n + 1 < end):
                            maxT(n + 1, at(1))
                        if mid or n + 3 < end:
                            if tau == 3:
                                xT(n + 3, at(3))
                            if tau == 6:
                                qk(n + 3, at(3))
                            if tau == 9:
                                v(n + 3, at(3))
                        if tau == 13 and (mid or n >= 1):
                            proj(n - 1, at(-1))
                        scores_t(n, r, tau)
                        if mid or n + 2 < end:
                            scores(n + 2, at(2), tau)
                        if tau == 3 and (mid or n >= 1):
                            pv(n - 1, at(-1), 3)
                        if tau % 4 == 3 and tau > 3:
                            pv(n, r, tau // 4 - 1)

                pe.wait_ge(s_wqk, 2)
                wait(pe, ffns[0].acca, NG)

                def prep(t):
                    xT(t, t)
                    qk(t, t)
                    v(t, t)
                prep(0)
                for tau in range(16):
                    scores(0, 0, tau)
                prep(1)
                for tau in range(16):
                    scores(1, 1, tau)
                    if tau == 1:
                        maxT(0, 0)
                prep(2)
                step(0, 0)
                with pe.Fori(0, 7) as i:
                    for r in range(NBUF):
                        step(4 * i + (r + 1), (r + 1) % NBUF)
                for n in (29, 30, 31):
                    step(n, n % NBUF)
                pv(NT - 1, (NT - 1) % NBUF, 3)
                proj(NT - 1, (NT - 1) % NBUF)

            ffn(ffns[0])
            attention()
            ffn(ffns[1])



_INS = ["L0_attn_x", "L0_attn_wq", "L0_attn_bq", "L0_attn_wk", "L0_attn_bk", "L0_attn_wv", "L0_attn_bv", "L0_attn_wo",
        "L0_attn_bo", "L0_attn_gamma", "L0_attn_beta", "L0_ffn_router_w", "L0_ffn_w_gate", "L0_ffn_w_up",
        "L0_ffn_w_down", "L0_ffn_ws_gate_up", "L0_ffn_ws_down"]


def kernel(**inputs):
    import numpy as np
    import concourse.bacc as bacc
    from concourse.bass_utils import run_bass_kernel_spmd

    nc = bacc.Bacc("TRN2", target_bir_lowering=False, num_devices=1)
    arrays, args = {}, []
    for name in _INS:
        a = np.ascontiguousarray(inputs[name])
        arrays[f"in_{name}"] = a
        args.append(nc.dram_tensor(f"in_{name}", a.shape, mybir.dt.from_np(a.dtype), kind="ExternalInput").ap())
    out = nc.dram_tensor("out_x", inputs["L0_attn_x"].shape, F32, kind="ExternalOutput").ap()
    macaron_kernel(nc, *args, out)
    r = run_bass_kernel_spmd(nc, [arrays], core_ids=[0])
    return r.results[0]["out_x"]
```

```python
from contextlib import ExitStack

import concourse.bass as bass
from concourse import mybir

F32 = mybir.dt.float32
BF16 = mybir.dt.bfloat16
U32 = mybir.dt.uint32
ALU = mybir.AluOpType
ACT = mybir.ActivationFunctionType
X = mybir.AxisListType.X
P = 128


def macaron_kernel(nc, x_in, wq, bq, wk, bk, wv, bv, wo, bo, gamma, beta,
                   router_w, w_gate, w_up, w_down, ws_gate_up, ws_down, out):
    B, S, D = x_in.shape
    T = B * S
    NT = T // P
    E, _, F = w_gate.shape
    K8, C = 8, 64
    NP2 = E // 2
    GT = 4
    NG = NT // GT
    NACC = 4
    ACC = T + C
    XW = D + E
    H, HD = 16, 8
    HS = S // H
    NH = P // HS
    NPART = 3
    NR = NPART * NPART * HD
    MR = P - 2
    SCALE = float(HD) ** -0.5
    LN_EPS = 1e-5
    NBUF = 4
    NPB = 8
    AW = 19072
    assert NH * HS == P and C * 2 == P and T % (P * GT) == 0

    x_rows = x_in.rearrange("b s d -> (b s) d")
    out_rows = out.rearrange("b s d -> (b s) d")
    xw_dram = [nc.dram_tensor(f"dispatch_rows{p}", [T, XW], F32, kind="Internal").ap() for p in range(2)]
    parts_dram = nc.dram_tensor("qk_parts", [4, 2 * NPART, P, P], BF16, kind="Internal").ap()
    ctx_dram = nc.dram_tensor("ctx", [4, P, 512], F32, kind="Internal").ap()
    acc_dram = [nc.dram_tensor(f"routed_sums{p}", [NACC * ACC, D], F32, kind="Internal").ap() for p in range(2)]

    with ExitStack() as ctx:
        def sb(name, shape, dt=F32):
            return ctx.enter_context(nc.sbuf_tensor(name, shape, dt))

        def sem(name):
            return ctx.enter_context(nc.semaphore(name))

        def wait(eng, s, value):
            if isinstance(s, Event):
                s, value = s.sem, value + s.base
            if isinstance(value, int) and value <= 0:
                return
            eng.wait_ge(s, value)

        def wait_each(eng, *waits):
            ready, taken = [], []
            for s, value in waits:
                if isinstance(s, Event):
                    s, value = s.sem, value + s.base
                if not isinstance(value, int):
                    count = eng.alloc_register()
                    eng.reg_mov(count, value)
                    taken.append(count)
                    value = count
                elif value <= 0:
                    continue
                ready.append((s, value))
            for s, value in ready:
                eng.wait_ge(s, value)
            for count in taken:
                eng.free_register(count)

        def wait_apart(eng, *waits):
            wait_each(eng, (s_cst, 1), *waits)

        x_sb = sb("x_sb", [P, NT, D])
        z_sb = sb("z_sb", [P, NT * D])
        xT_all = z_sb[:]
        wg_sb = sb("wg_sb", [P, E, F])
        wu_sb = sb("wu_sb", [P, E, F])
        wd_sb = sb("wd_sb", [F, E, D])
        wsgu_sb = sb("wsgu_sb", [P, 2 * F])
        wsd_sb = sb("wsd_sb", [F, D])
        rw_sb = sb("rw_sb", [E, D])
        rwT = sb("rwT", [P, E])
        ident = sb("ident", [P, P])
        identb = sb("identb", [P, P], BF16)
        zeros = sb("zeros", [P, 10 * D])
        keyt = sb("keyt", [P, NT])
        slot_c = sb("slot_c", [P, 1])
        acc_off = sb("acc_off", [P, NP2])
        stats = sb("stats", [P, NT, 6])
        mv = sb("mv", [P, NT, 2])
        rstd = sb("rstd", [P, NT])
        xn_sb = sb("xn_sb", [P, 2, GT, D])
        arena = sb("arena", [P, AW])

        used = [0]

        def carve(words, start=None):
            if start is not None:
                used[0] = start
            a = used[0]
            used[0] += words
            assert used[0] <= AW, used[0]
            return arena[:, a:a + words]

        xT_r = [carve(GT * P) for _ in range(2)]
        d_r = [carve(GT * E) for _ in range(2)]
        e_r = [carve(GT * E) for _ in range(2)]
        top_r = [carve(GT * K8) for _ in range(2)]
        w_r = [carve(GT * E) for _ in range(2)]
        m_r = [carve(GT) for _ in range(2)]
        den_r = [carve(GT) for _ in range(2)]
        key = carve(NT * E)
        KT = carve(NT * E)
        cand = carve(C)
        merged = carve(2 * C)
        slots = carve(C)
        kc = carve(NP2)
        tokf = carve(NP2)
        emp = carve(NP2)
        gidx = carve(NP2).bitcast(U32)
        sidx = carve(NP2).bitcast(U32)
        NGB = 16
        gat = [carve(XW) for _ in range(NGB)]
        gT = [carve(2 * P) for _ in range(2)]
        sil = [carve(4 * C) for _ in range(2)]
        hid = [carve(4 * C) for _ in range(2)]
        NYB = 4
        y_r = [carve(D) for _ in range(NYB)]
        acc_r = [carve(GT * D) for _ in range(2 * NACC)]
        shs = [xT_r[0], xT_r[1]]
        shu = [acc_r[0], acc_r[1]]
        shy = [acc_r[2], acc_r[3]]
        shh = [carve(GT * P) for _ in range(2)]

        QC = H * P
        q_st = [carve(QC // 2, 0 if i == 0 else None).bitcast(BF16) for i in range(NBUF)]
        k_st = [carve(QC // 2).bitcast(BF16) for i in range(NBUF)]
        p_r = [carve(H * HS) for _ in range(NPB)]
        v_all = carve(NBUF * NH * 4 * 32)
        v_r = [v_all[:, i * NH * 128:(i + 1) * NH * 128].rearrange("p (g k c) -> p g k c", g=NH, k=4) for i in range(NBUF)]
        xn_r = [carve(P) for _ in range(2)]
        xTt_r = [carve(P) for _ in range(2)]
        qk_r = [carve(2 * P) for _ in range(2)]
        res_r = [carve(2 * P) for _ in range(2)]
        part_r = [carve(3 * P).bitcast(BF16) for _ in range(2)]
        ctx_r = [carve(H * HS) for _ in range(2)]
        num_r = [carve(P) for _ in range(2)]
        den2_r = [carve(P) for _ in range(2)]
        cT_r = [carve(P) for _ in range(2)]
        mx_r = [carve(NH * 4) for _ in range(2)]
        mhl_r = [carve(NH * 4).bitcast(BF16) for _ in range(2)]
        mT_r = [carve(2 * P).bitcast(BF16)[0:8, :] for _ in range(2)]

        def heads(stack, rows, g):
            return stack[rows, :].rearrange("r (c g) -> r c g", g=NH)[:, :, g]

        wqk_raw = sb("wqk_raw", [P, 2 * D])
        wqk_sb = sb("wqk_sb", [P, 2 * D])
        wv_sb = sb("wv_sb", [P, D])
        wo_sb = sb("wo_sb", [P, D])
        bqk_sb = sb("bqk_sb", [P, 2])
        bv_sb = sb("bv_sb", [P, 32])
        bo_sb = sb("bo_sb", [P, D])
        gamma_sb = sb("gamma_sb", [P, D])
        beta_sb = sb("beta_sb", [P, D])
        statz = sb("statz", [P, NT, 6])
        mvz = sb("mvz", [P, NT, 2])
        rstdz = sb("rstdz", [P, NT])

        psum = ctx.enter_context(nc.psum_tensor("psum", [P, 8 * 512], F32))
        bank = [psum[:, i * 512:(i + 1) * 512] for i in range(8)]

        s_ld = sem("s_ld")
        s_x = sem("x_loaded")
        s_wr = sem("router_loaded")
        s_wsh = sem("shared_loaded")
        s_wexp = sem("experts_loaded")
        s_cst = sem("constants_ready")
        s_cst1 = sem("constants_step")
        s_zero = sem("zeros_ready")
        s_rwp = sem("router_transposed")
        s_rws = sem("router_copied")
        s_acc0 = [sem(f"sums_zeroed{p}") for p in range(2)]
        s_xfin = [sem(f"x_after_ffn{p}") for p in range(2)]
        s_out = sem("out_stored")

        totals = dict(stats_done=NT, var_ready=NT, eps_added=1, std_ready=1, rstd_ready=1,
                      xn_ready=NG, xT_in_psum=NG, xT_copied=2 * NG, logits_in_psum=NG, row_max=NG, shifted_logits=NT,
                      top8_found=NT, top8_marked=NT, keys_ready=NG, exp_ready=NG, masked_exp=NG, exp_sum=NG,
                      exp_recip=NG, weights_ready=NG, keys_transposed=4, keys_copied=4, list_step=38,
                      slots_transposed=1, indices_ready=1, shared_up_in_psum=NG, shared_up_copied=NG, shared_silu=NG, shared_hidden=NG,
                      shared_out_in_psum=NG, shared_out_copied=NG, shared_added=NG, x_centered=NG, slotsT_in_psum=NP2 // 2, slotsT_copied=NP2 // 2,
                      gate_up_in_psum=NP2 // 2, silu_ready=NP2 // 2, hidden_ready=NP2 // 2, y_in_psum=NP2 // 2,
                      y_weighted=2 * NP2, sums_step=(NACC - 1) * NG, sums_added=NG)
        for i in range(2):
            totals[f"xn_stored{i}"] = totals[f"weights_stored{i}"] = 16 * NG // 2
            totals[f"scattered{i}"] = 16 * NP2 // 2
            totals[f"sums_loaded{i}"] = 16 * NACC * NG // 2
        for i in range(NGB):
            totals[f"gathered{i}"] = 16 * NP2 // NGB
        ffn_sems = {name: sem(name) for name in totals}

        class Event:

            def __init__(self, name, p):
                self.sem, self.base = ffn_sems[name], p * totals[name]

        class Ffn:

            def __init__(self, p):
                n = lambda s: Event(s, p)
                self.p = p
                self.stat, self.aggr, self.sd, self.rs = n("stats_done"), n("var_ready"), n("std_ready"), n("rstd_ready")
                self.ve = n("eps_added")
                self.xn, self.xtp, self.xts = n("xn_ready"), n("xT_in_psum"), n("xT_copied")
                self.lg, self.mx, self.d = n("logits_in_psum"), n("row_max"), n("shifted_logits")
                self.top, self.rep, self.key = n("top8_found"), n("top8_marked"), n("keys_ready")
                self.ex, self.es, self.den = n("exp_ready"), n("masked_exp"), n("exp_sum")
                self.rden, self.w = n("exp_recip"), n("weights_ready")
                self.cen = n("x_centered")
                self.xns = [n(f"xn_stored{i}") for i in range(2)]
                self.ws = [n(f"weights_stored{i}") for i in range(2)]
                self.ktp, self.kts = n("keys_transposed"), n("keys_copied")
                self.rnd = n("list_step")
                self.slp = n("slots_transposed")
                self.idx = n("indices_ready")
                self.shp, self.shs, self.shh = n("shared_up_in_psum"), n("shared_silu"), n("shared_hidden")
                self.shc = n("shared_up_copied")
                self.sho, self.shy, self.shx = n("shared_out_in_psum"), n("shared_out_copied"), n("shared_added")
                self.gat = [n(f"gathered{i}") for i in range(NGB)]
                self.gtp, self.gts = n("slotsT_in_psum"), n("slotsT_copied")
                self.gu, self.sil, self.hid = n("gate_up_in_psum"), n("silu_ready"), n("hidden_ready")
                self.y, self.ys = n("y_in_psum"), n("y_weighted")
                self.sca = [n(f"scattered{i}") for i in range(2)]
                self.accl = [n(f"sums_loaded{i}") for i in range(2)]
                self.add, self.acca = n("sums_step"), n("sums_added")

        ffns = [Ffn(0), Ffn(1)]
        s_watt = sem("att_weights_loaded")
        s_wqk = sem("wqk_permuted")
        s_vini = sem("v_ring_filled")
        s_vst = sem("v_ring_step")
        a_stat, a_aggr, a_ve, a_sd, a_rs = sem("a_stats"), sem("a_var"), sem("a_eps"), sem("a_std"), sem("a_rstd")
        a_xn = sem("a_xn_ready")
        a_zb = sem("a_residual_ready")
        a_xb = sem("a_x_plus_beta")
        a_use = sem("a_misc_written")
        a_read = sem("a_misc_read")
        a_part1, a_res1, a_part2, a_parts = sem("a_part1"), sem("a_rest1"), sem("a_part2"), sem("a_parts_ready")
        a_stk = [sem(f"a_stack_loaded{i}") for i in range(NBUF)]
        a_mrow = [sem(f"a_max_rows_loaded{i}") for i in range(NBUF)]
        a_S, a_mx = sem("a_scores_in_psum"), sem("a_max_ready")
        a_pst, a_cst = sem("a_parts_stored"), sem("a_ctx_stored")
        a_hi, a_hl = sem("a_max_high"), sem("a_max_split")
        a_ST, a_P, a_PV = sem("a_scoresT_in_psum"), sem("a_exp_ready"), sem("a_pv_done")
        a_cx = sem("a_ctx_copied")
        a_cd = [sem(f"a_ctx_moved{i}") for i in range(2)]
        a_rc, a_ct = sem("a_recip"), sem("a_ctxT_ready")
        a_zs, a_za = sem("a_z_stats"), sem("a_z_var")
        a_zve, a_zsd, a_zrs = sem("a_z_eps"), sem("a_z_std"), sem("a_z_rstd")
        a_fin1, a_fin = sem("a_final_scaled"), sem("a_final_added")

        uses = [("x", 0), ("q", 0), ("v", 0), ("x", 1), ("q", 1), ("v", 1), ("m", 0), ("x", 2), ("q", 2), ("v", 2),
                ("x", 3), ("q", 3)]
        for n in range(NT + 2):
            uses += [u for u in (("x", n + 4), ("m", n + 1), ("q", n + 4), ("v", n + 3), ("o", n - 2))
                     if 0 <= u[1] < NT]
        where = {u: i for i, u in enumerate(uses)}

        def use(kind, t):
            if isinstance(t, int):
                return where[kind, t]
            return 5 * t + (where[kind, 10] - 50)

        def lap(n, r, ring, per):
            return n * (per // ring) + (per - r * (per // ring))

        block = ctx.enter_context(nc.Block())

        @block.sync
        def _(sp):
            sp.dma_start(x_sb[:], x_rows.rearrange("(i p) d -> p i d", p=P)).then_inc(s_x, 16)
            sp.dma_start(rw_sb[:], router_w).then_inc(s_wr, 16)
            sp.dma_start(wsgu_sb[:], ws_gate_up).then_inc(s_wsh, 16)
            sp.dma_start(wsd_sb[:], ws_down).then_inc(s_wsh, 16)
            sp.wait_ge(s_zero, 1)

            def zero_sums(p, part=0, parts=1):
                z = acc_dram[p].rearrange("(c p r) d -> c p (r d)", p=P, r=10)
                for c in range(part, z.shape[0], parts):
                    sp.dma_start(z[c], zeros[:]).then_inc(s_acc0[p], 16)

            sp.dma_start(wv_sb[:], wv).then_inc(s_watt, 16)
            sp.dma_start(wo_sb[:], wo.rearrange("(j d) n -> d j n", d=HD)).then_inc(s_watt, 16)
            for i, (w, b) in enumerate(((wq, bq), (wk, bk))):
                sp.dma_start(wqk_raw[:, i * D:(i + 1) * D], w).then_inc(s_watt, 16)
                sp.dma_start(bqk_sb[:, i:i + 1], b.rearrange("(j d o) -> d j o", d=HD, o=1), allow_slow_non_contiguous=True).then_inc(s_watt, 16)
            for jj in range(4):
                sp.dma_start(bv_sb[jj * 32:(jj + 1) * 32, :].rearrange("p (k d) -> p k d", k=4),
                             bv.rearrange("(o k jj d) -> jj o k d", o=1, k=4, jj=4)[jj].to_broadcast([32, 4, HD]))\
                  .then_inc(s_watt, 16)
            for t, b in ((bo_sb, bo), (gamma_sb, gamma), (beta_sb, beta)):
                sp.dma_start(t[:], b.rearrange("(o c) -> o c", o=1).to_broadcast([P, D])).then_inc(s_watt, 16)
            zero_sums(0)

            def ffn(f):
                rows = xw_dram[f.p].rearrange("(i p) c -> p i c", p=P)

                def store(g, r):
                    wait(sp, f.xn, g + 1)
                    sp.dma_start(rows[:, bass.ds(g * GT, GT), 0:D], xn_sb[:, r, :, :]).then_inc(f.xns[r].sem, 16)

                def store_w(g, r):
                    wait(sp, f.w, g + 1)
                    sp.dma_start(rows[:, bass.ds(g * GT, GT), D:XW], w_r[r].rearrange("p (i e) -> p i e", i=GT))\
                      .then_inc(f.ws[r].sem, 16)
                store(0, 0)
                store(1, 1)
                store_w(0, 0)
                with sp.Fori(1, NG // 2) as i:
                    for r in range(2):
                        store(2 * i + r, r)
                        store_w(2 * i + (r - 1), 1 - r)
                store_w(NG - 1, 1)
                if f.p == 0:
                    for w, t in ((w_gate, wg_sb), (w_up, wu_sb), (w_down, wd_sb)):
                        sp.dma_start(t[:], w.rearrange("e k n -> k e n")).then_inc(s_wexp, 16)
                wait(sp, f.shx, NG)
                wait(sp, f.sca[0], 16 * (NP2 // 2))
                wait(sp, f.sca[1], 16 * (NP2 // 2))
                accs = acc_dram[f.p].rearrange("(a t) d -> a t d", a=NACC)[:, 0:T, :].rearrange("a (i p) d -> a p i d", p=P)

                def load(g, r):
                    wait(sp, f.acca, g - 1)
                    for a in range(NACC):
                        sp.dma_start(acc_r[r * NACC + a].rearrange("p (i d) -> p i d", i=GT),
                                     accs[a, :, bass.ds(g * GT, GT), :]).then_inc(f.accl[r].sem, 16)
                load(0, 0)
                load(1, 1)
                with sp.Fori(1, NG // 2) as i:
                    for r in range(2):
                        load(2 * i + r, r)

            def attention():
                def max_rows(t, r):
                    sp.wait_ge(a_read, use("m", t) + 1)
                    sp.dma_start(q_st[r][MR:P, :].rearrange("h (q c) -> h q c", q=4), mT_r[r % 2])\
                      .then_inc(a_mrow[r], 16)

                def stack_store(t, r):
                    sp.wait_ge(a_parts, t + 1)
                    sp.dma_start(parts_dram[r].rearrange("c p t -> p c t"),
                                 part_r[r % 2].rearrange("p (c t) -> p c t", t=P)).then_inc(a_pst, 16)

                def stack_load(t, r):
                    wait_each(sp, (a_ST, 16 * (t - 3)), (a_pst, 16 * t + 16))
                    parts = parts_dram[r].rearrange("c p t -> c (p t)")
                    for a in range(NPART):
                        rows = slice(a * NPART * HD, (a + 1) * NPART * HD)
                        sp.dma_start(q_st[r][rows, :], parts[a:a + 1].to_broadcast([NPART, P * P])).then_inc(a_stk[r], 16)
                    sp.dma_start(k_st[r][0:NR, :], parts[NPART:2 * NPART].rearrange("(o c) x -> o (c x)", o=1)
                                 .to_broadcast([NPART, NPART * P * P])).then_inc(a_stk[r], 16)

                def ctx_store(t, r):
                    sp.wait_ge(a_cx, t + 1)
                    sp.dma_start(ctx_dram[r], ctx_r[r % 2]).then_inc(a_cst, 16)

                def ctx_load(t, r):
                    wait_each(sp, (a_use, use("o", t - 2) + 1 if not isinstance(t, int) or t >= 2 else 0),
                              (a_cst, 16 * t + 16))
                    for k, dst in enumerate((num_r, den2_r)):
                        src = ctx_dram[r].rearrange("(g x) c -> g (x c)", g=NH)[:, k * HD * 512:(k + 1) * HD * 512]
                        sp.dma_start(dst[r % 2].rearrange("p (g s) -> p g s", g=NH),
                                     src.rearrange("g (p s) -> p g s", s=HS)).then_inc(a_cd[r % 2], 16)

                sp.wait_ge(s_vini, 2)
                for t in range(3):
                    stack_store(t, t)
                    stack_load(t, t)
                    if t == 1:
                        max_rows(0, 0)
                stack_store(3, 3)
                def step(n, r, end=NT):
                    mid = not isinstance(n, int)
                    if mid or n + 3 < end:
                        stack_load(n + 3, (r + 3) % NBUF)
                    if mid or n + 1 < end:
                        max_rows(n + 1, (r + 1) % NBUF)
                    if mid or n >= 1:
                        ctx_store(n - 1, (r - 1) % NBUF)
                    if mid or n + 4 < end:
                        stack_store(n + 4, r)
                    if mid or n >= 1:
                        ctx_load(n - 1, (r - 1) % NBUF)
                for n in range(NBUF):
                    step(n, n)
                    zero_sums(1, n, NBUF)
                with sp.Fori(1, NT // NBUF - 1) as i:
                    for r in range(NBUF):
                        step(NBUF * i + r, r)
                for n in range(NT - NBUF, NT):
                    step(n, n % NBUF)
                ctx_store(NT - 1, (NT - 1) % NBUF)
                ctx_load(NT - 1, (NT - 1) % NBUF)

            ffn(ffns[0])
            attention()
            ffn(ffns[1])
            wait(sp, ffns[1].acca, NG)
            sp.dma_start(out_rows.rearrange("(i p) d -> p i d", p=P), x_sb[:]).then_inc(s_out, 16)
            sp.wait_ge(s_out, 16)

        @block.gpsimd
        def _(pool):
            pool.memset(zeros[:], 0.0).then_inc(s_zero, 1)
            pool.memset(ident[:], 0.0).then_inc(s_cst1, 1)
            pool.memset(identb[:], 0.0).then_inc(s_cst1, 1)
            pool.wait_ge(s_cst1, 2)
            for t in (ident, identb):
                pool.affine_select(out=t[:], in_=t[:], compare_op=ALU.not_equal, fill=1.0, base=0,
                                   pattern=[[-1, P]], channel_multiplier=1).then_inc(s_cst, 1)
            f32 = dict(allow_small_or_imprecise_dtypes=True)
            pool.iota(keyt[:], pattern=[[-P, NT]], base=T, channel_multiplier=-1, **f32).then_inc(s_cst, 1)
            for half in range(2):
                rows = slice(half * C, (half + 1) * C)
                pool.wait_ge(s_cst, 3 + 2 * half)
                pool.iota(slot_c[rows, :], pattern=[[0, 1]], base=0, channel_multiplier=1, **f32).then_inc(s_cst, 1)
                pool.iota(acc_off[rows, :], pattern=[[0, NP2 // 2], [2 * ACC, 2]], base=half * ACC,
                          channel_multiplier=0, **f32).then_inc(s_cst, 1)

            def ffn(f):
                def normalise(g, r):
                    xn = xn_sb[:, r, :, :]
                    wait(pool, f.xns[r], 16 * ((g - r) // 2) if isinstance(g, int) else 8 * (g - r))
                    wait(pool, f.xtp, g - 1)
                    pool.tensor_tensor(xn, x_sb[:, bass.ds(g * GT, GT), :],
                                       mv[:, bass.ds(g * GT, GT), 0:1].to_broadcast([P, GT, D]),
                                       ALU.subtract).then_inc(f.cen.sem, 1)
                    wait(pool, f.cen, g + 1)
                    pool.tensor_tensor(xn, xn, rstd[:, bass.ds(g * GT, GT)].unsqueeze(2).to_broadcast([P, GT, D]),
                                       ALU.mult).then_inc(f.xn.sem, 1)
                pool.wait_ge(s_cst, 7)
                wait(pool, f.rs, 1)
                normalise(0, 0)
                normalise(1, 1)
                with pool.Fori(1, NG // 2) as i:
                    for r in range(2):
                        normalise(2 * i + r, r)

                def shared_mul(g, r):
                    wait(pool, f.shx, g - 1)
                    wait(pool, f.shs, g + 1)
                    wait(pool, f.shc, g + 1)
                    wait(pool, f.sho, g - 1)
                    pool.tensor_tensor(shh[r][0:F, :], shs[r][0:F, :], shu[r][0:F, :], ALU.mult).then_inc(f.shh.sem, 1)

                def shared_add(g, r):
                    wait(pool, f.shh, g + 2 if not isinstance(g, int) or g + 2 < NG else NG)
                    wait(pool, f.shy, g + 1)
                    xs = x_sb[:, bass.ds(g * GT, GT), :]
                    pool.tensor_tensor(xs, xs, shy[r].rearrange("p (i d) -> p i d", i=GT), ALU.add).then_inc(f.shx.sem, 1)
                shared_mul(0, 0)
                shared_mul(1, 1)
                shared_add(0, 0)
                with pool.Fori(1, NG // 2) as i:
                    for r in range(2):
                        shared_mul(2 * i + r, r)
                        shared_add(2 * i + (r - 1), 1 - r)
                shared_add(NG - 1, 1)

                wait(pool, f.shx, NG)
                wait(pool, f.idx, 1)
                for r in range(2):
                    wait(pool, f.xns[r], 16 * (NG // 2))
                    wait(pool, f.ws[r], 16 * (NG // 2))
                pool.wait_ge(s_acc0[f.p], 16 * (NACC * ACC // (P * 10)))

                def gather(k):
                    wait(pool, f.ys, 4 * ((k - NGB) // 2 + 1) if k >= NGB else 0)
                    pool.indirect_dma_start(out=gat[k % NGB], out_offset=None, in_=xw_dram[f.p],
                                            in_offset=bass.IndirectOffsetOnAxis(ap=gidx[:, k:k + 1], axis=0),
                                            ).then_inc(f.gat[k % NGB].sem, 16)

                LEAD = 12
                for k in range(LEAD):
                    gather(k)
                for k in range(NP2):
                    if k + LEAD < NP2:
                        gather(k + LEAD)
                    wait(pool, f.ys, 4 * (k // 2) + 2 * (k % 2) + 2)
                    wait(pool, f.sca[k % 2], 16 * (k // 2))
                    pool.indirect_dma_start(out=acc_dram[f.p], in_=y_r[k % NYB], in_offset=None,
                                            out_offset=bass.IndirectOffsetOnAxis(ap=sidx[:, k:k + 1], axis=0),
                                            compute_op=ALU.add).then_inc(f.sca[k % 2].sem, 16)

            def attention():
                wait(pool, ffns[0].acca, NG)
                pool.memset(v_all, 0.0).then_inc(s_vst, 1)
                pool.wait_ge(s_vst, 1)
                pool.memset(v_all.rearrange("p (a c) -> p a c", c=32)[:, :, HD:2 * HD], 1.0).then_inc(s_vini, 1)
                for i in range(NBUF):
                    pool.memset(q_st[i][:, :], 0.0)
                    ins = pool.memset(k_st[i][:, :], -1.0)
                ins.then_inc(s_vini, 1)
                pool.wait_ge(s_vini, 2)
                pool.wait_ge(s_watt, 16 * 13)

                def prep(t, r):
                    xt = x_sb[:, bass.ds(t, 1), :].rearrange("p a d -> p (a d)")
                    pool.wait_ge(a_xn, t + 1)
                    pool.tensor_tensor(z_sb[:, bass.ds(t * P, P)], xn_r[r % 2], bo_sb[:], ALU.add).then_inc(a_zb, 1)
                    pool.tensor_tensor(xt, xt, beta_sb[:], ALU.add).then_inc(a_xb, 1)
                    p1, p2, p3 = [part_r[r % 2].rearrange("p (qk c t) -> p c qk t", qk=2, c=3)[:, c] for c in range(3)]
                    qk, res = [b[r % 2].rearrange("p (qk t) -> p qk t", qk=2) for b in (qk_r, res_r)]
                    waits = [(a_read, use("q", t) + 1)]
                    if not isinstance(t, int) or t >= 2:
                        waits.append((a_pst, 16 * (t - 1)))
                    wait_apart(pool, *waits)
                    pool.tensor_copy(p1, qk).then_inc(a_part1, 1)
                    pool.wait_ge(a_part1, t + 1)
                    pool.tensor_tensor(res, qk, p1, ALU.subtract).then_inc(a_res1, 1)
                    wait_apart(pool, (a_res1, t + 1))
                    pool.tensor_copy(p2, res).then_inc(a_part2, 1)
                    pool.wait_ge(a_part2, t + 1)
                    pool.tensor_tensor(p3, res, p2, ALU.subtract).then_inc(a_parts, 1)

                for t in range(2 * NBUF):
                    prep(t, t % NBUF)
                with pool.Fori(2, NT // NBUF) as i:
                    for r in range(NBUF):
                        prep(NBUF * i + r, r)

            ffn(ffns[0])
            attention()
            ffn(ffns[1])

        @block.vector
        def _(dve):
            def layernorm_stats(f_stat, f_aggr, f_ve, f_sd, f_rs):
                inc = lambda ins, s: ins.then_inc(s.sem if isinstance(s, Event) else s, 1)
                for i in range(NT):
                    inc(dve.bn_stats(stats[:, i, :], x_sb[:, i, :]), f_stat)
                for i in range(NT):
                    wait(dve, f_stat, i + 1)
                    inc(dve.bn_aggr(mv[:, i, :], stats[:, i, :]), f_aggr)
                wait(dve, f_aggr, NT)
                inc(dve.tensor_scalar(rstd[:], mv[:, :, 1], LN_EPS, None, ALU.add), f_ve)
                wait(dve, f_sd, 1)
                inc(dve.reciprocal(rstd[:], rstd[:]), f_rs)
                wait(dve, f_rs, 1)

            def ffn(f):
                layernorm_stats(f.stat, f.aggr, f.ve, f.sd, f.rs)

                def route(g, r):
                    lg = bank[2 + r][:, 0:GT * E].rearrange("p (j e) -> p j e", j=GT)
                    d = d_r[r].rearrange("p (j e) -> p j e", j=GT)
                    e = e_r[r].rearrange("p (j e) -> p j e", j=GT)
                    top = top_r[r].rearrange("p (j e) -> p j e", j=GT)
                    kk = key.rearrange("p (i e) -> p i e", e=E)
                    wait(dve, f.lg, g + 1)
                    dve.tensor_reduce(m_r[r], lg, X, ALU.max).then_inc(f.mx.sem, 1)
                    wait(dve, f.mx, g + 1)
                    for j in range(GT):
                        dve.tensor_scalar(d[:, j, :], lg[:, j, :], m_r[r][:, j:j + 1], -88.0,
                                          ALU.subtract, ALU.max).then_inc(f.d.sem, 1)
                    for j in range(GT):
                        wait_apart(dve, (f.d, g * GT + j + 1))
                        dve.max(top[:, j, :], d[:, j, :]).then_inc(f.top.sem, 1)
                    for j in range(GT):
                        wait_apart(dve, (f.top, g * GT + j + 1), (f.ex, g + 1))
                        dve.match_replace(d[:, j, :], top[:, j, :], d[:, j, :], 1.0).then_inc(f.rep.sem, 1)
                    wait(dve, f.rep, GT * (g + 1))
                    dve.scalar_tensor_tensor(out=kk[:, bass.ds(g * GT, GT), :], in0=d, scalar=0.5,
                                             in1=keyt[:, bass.ds(g * GT, GT)].unsqueeze(2).to_broadcast([P, GT, E]),
                                             op0=ALU.is_gt, op1=ALU.mult).then_inc(f.key.sem, 1)
                    dve.scalar_tensor_tensor(out=e_r[r], in0=d_r[r], scalar=0.5, in1=e_r[r],
                                             op0=ALU.is_gt, op1=ALU.mult).then_inc(f.es.sem, 1)
                    wait(dve, f.es, g + 1)
                    dve.tensor_reduce(den_r[r], e, X, ALU.add).then_inc(f.den.sem, 1)
                    wait(dve, f.den, g + 1)
                    dve.reciprocal(den_r[r], den_r[r]).then_inc(f.rden.sem, 1)
                    wait(dve, f.rden, g + 1)
                    wait(dve, f.ws[r], 16 * ((g - r) // 2) if isinstance(g, int) else 8 * (g - r))
                    dve.scalar_tensor_tensor(out=w_r[r].rearrange("p (j e) -> p j e", j=GT), in0=e, scalar=0.5,
                                             in1=den_r[r].unsqueeze(2).to_broadcast([P, GT, E]),
                                             op0=ALU.mult, op1=ALU.mult).then_inc(f.w.sem, 1)

                dve.wait_ge(s_cst, 7)
                route(0, 0)
                route(1, 1)
                with dve.Fori(1, NG // 2) as i:
                    for r in range(2):
                        route(2 * i + r, r)

                step = [0]

                def link(ins):
                    step[0] += 1
                    ins.then_inc(f.rnd.sem, 1)
                    wait(dve, f.rnd, step[0])

                def top_list(dst, src):
                    for c in range(0, C, 8):
                        link(dve.max(dst[:, c:c + 8], src))
                        if c + 8 < C:
                            link(dve.match_replace(src, dst[:, c:c + 8], src, 0.0))

                wait(dve, f.kts, 4)
                top_list(cand, KT)
                link(dve.tensor_copy(merged[0:E, 0:C], cand[0:E, :]))
                link(dve.tensor_copy(merged[0:E, C:2 * C], cand[E:2 * E, :]))
                top_list(slots[0:E, :], merged[0:E, :])
                wait(dve, f.slp, 1)
                both = bank[6][0:C, 0:E].rearrange("c (k two) -> c k two", two=2)
                link(dve.tensor_copy(kc[0:C, :], both[:, :, 0]))
                link(dve.tensor_copy(kc[C:P, :], both[:, :, 1]))
                link(dve.tensor_scalar(tokf, kc, -1.0, float(T), ALU.mult, ALU.add))
                link(dve.tensor_scalar(gidx, tokf, float(T - 1), None, ALU.min))
                link(dve.tensor_scalar(emp, kc, 0.0, slot_c[:, 0:1], ALU.is_equal, ALU.mult))
                link(dve.tensor_tensor(emp, emp, acc_off[:], ALU.add))
                dve.tensor_tensor(sidx, tokf, emp, ALU.add).then_inc(f.idx.sem, 1)

                def hidden(q):
                    r = q % 2
                    wait(dve, f.sil, q + 1)
                    wait(dve, f.y, q - 1)
                    dve.tensor_tensor(hid[r][0:F, :], sil[r][0:F, :], bank[2 + r][0:F, 4 * C:8 * C],
                                      ALU.mult).then_inc(f.hid.sem, 1)
                hidden(0)
                for q in range(NP2 // 2):
                    r = q % 2
                    if q + 1 < NP2 // 2:
                        hidden(q + 1)
                    wait(dve, f.y, q + 1)
                    for j in range(2):
                        k = 2 * q + j
                        wait(dve, f.sca[k % 2], 16 * ((k - NYB) // 2 + 1) if k >= NYB else 0)
                        for half in range(2):
                            rows = slice(half * C, (half + 1) * C)
                            col = D + 2 * k + half
                            dve.tensor_scalar(y_r[k % NYB][rows, :], bank[4 + r][rows, j * D:(j + 1) * D],
                                              gat[k % NGB][rows, col:col + 1], None, ALU.mult).then_inc(f.ys.sem, 1)

                def add(g, r):
                    xs = x_sb[:, bass.ds(g * GT, GT), :]
                    for a in range(NACC):
                        if a == 0:
                            wait(dve, f.accl[r], 16 * NACC * ((g - r) // 2 + 1) if isinstance(g, int)
                                        else 8 * NACC * (g - r) + 16 * NACC)
                        else:
                            wait(dve, f.add, (g * (NACC - 1)) + a)
                        src = acc_r[r * NACC + a].rearrange("p (i d) -> p i d", i=GT)
                        ins = dve.tensor_tensor(xs, xs, src, ALU.add)
                        ins.then_inc((f.add if a < NACC - 1 else f.acca).sem, 1)
                with dve.Fori(0, NG // 2) as i:
                    for r in range(2):
                        add(2 * i + r, r)
                wait(dve, f.acca, NG)

            def attention():
                dve.wait_ge(s_watt, 16 * 13)
                for i in range(2):
                    dve.tensor_copy(wqk_sb[:, i * D:(i + 1) * D].rearrange("k (d j) -> k d j", d=HD),
                                    wqk_raw[:, i * D:(i + 1) * D].rearrange("k (j d) -> k d j", d=HD)).then_inc(s_wqk, 1)
                layernorm_stats(a_stat, a_aggr, a_ve, a_sd, a_rs)

                def xn(t, r):
                    if not isinstance(t, int) or t >= 2:
                        dve.wait_ge(a_zb, t - 1)
                        dve.wait_ge(a_use, use("x", t - 2) + 1)
                    dve.tensor_scalar(xn_r[r % 2], x_sb[:, bass.ds(t, 1), :].rearrange("p a d -> p (a d)"),
                                      mv[:, bass.ds(t, 1), 0], rstd[:, bass.ds(t, 1)],
                                      ALU.subtract, ALU.mult).then_inc(a_xn, 1)

                def v_copy(t, r):
                    dve.wait_ge(a_use, use("v", t) + 1)
                    wait(dve, a_PV, 4 * (t - 3))
                    b = bv_sb[:].rearrange("p (k c) -> p k c", k=4).unsqueeze(1).to_broadcast([P, NH, 4, HD])
                    dve.tensor_tensor(v_r[r][:, :, :, 0:HD], bank[7][:, 0:P].rearrange("p (g k c) -> p g k c", g=NH, k=4),
                                      b, ALU.add).then_inc(a_read, 1)

                def row_max(t, r, p):
                    dve.wait_ge(a_S, 8 * t + (p + 1))
                    src = psum[:, (p % 2) * 1024:(p % 2) * 1024 + 1024].rearrange("p (a k) -> p a k", a=2)
                    dve.tensor_reduce(mx_r[r % 2][:, 2 * p:2 * p + 2], src, X, ALU.max).then_inc(a_mx, 1)

                def max_high(t, r):
                    dve.wait_ge(a_mx, 8 * t + 8)
                    hl = mhl_r[r % 2].rearrange("p (g h q) -> p g h q", g=NH, h=2)
                    mx = mx_r[r % 2].rearrange("p (g q) -> p g q", g=NH)
                    dve.tensor_copy(hl[:, :, 0, :], mx).then_inc(a_hi, 1)

                def max_low(t, r):
                    dve.wait_ge(a_hi, t + 1)
                    hl = mhl_r[r % 2].rearrange("p (g h q) -> p g h q", g=NH, h=2)
                    mx = mx_r[r % 2].rearrange("p (g q) -> p g q", g=NH)
                    dve.tensor_tensor(hl[:, :, 1, :], mx, hl[:, :, 0, :], ALU.subtract).then_inc(a_hl, 1)

                def max_copy(t, r):
                    dve.wait_ge(a_use, use("m", t) + 1)
                    if not isinstance(t, int) or t >= 2:
                        dve.wait_ge(a_mrow[(r - 2) % NBUF], lap(t - 2, (r - 2) % NBUF, NBUF, 16))
                    dve.tensor_copy(mT_r[r % 2].rearrange("m (c g) -> m g c", g=NH),
                                    bank[7][0:8, 0:2 * P].bitcast(BF16).rearrange("m (g c) -> m g c", g=NH))\
                       .then_inc(a_read, 1)

                def ctx_recip(t, r):
                    dve.wait_ge(a_cd[r % 2], lap(t, r % 2, 2, 16 * 2))
                    dve.reciprocal(den2_r[r % 2], den2_r[r % 2]).then_inc(a_rc, 1)

                def ctx_div(t, r):
                    dve.wait_ge(a_rc, t + 1)
                    wait(dve, a_use, use("o", t - 2) + 1 if not isinstance(t, int) or t >= 2 else 0)
                    dve.tensor_tensor(cT_r[r % 2], num_r[r % 2], den2_r[r % 2], ALU.mult).then_inc(a_ct, 1)

                def z_add(t):
                    dve.wait_ge(a_use, use("o", t) + 1)
                    dve.wait_ge(a_zb, t + 1)
                    z = z_sb[:, bass.ds(t * P, P)]
                    dve.tensor_tensor(z, bank[7][:, 0:P], z, ALU.add).then_inc(a_read, 1)

                def z_stats(t):
                    dve.wait_ge(a_read, use("o", t) + 1)
                    dve.bn_stats(statz[:, bass.ds(t, 1), :].rearrange("p a c -> p (a c)"),
                                 z_sb[:, bass.ds(t * P, P)]).then_inc(a_zs, 1)

                xn(0, 0)
                xn(1, 1)
                dve.wait_ge(s_vini, 2)
                v_copy(0, 0)
                for p in range(8):
                    row_max(0, 0, p)
                max_high(0, 0)
                max_low(0, 0)
                xn(2, 2)
                v_copy(1, 1)
                for p in range(8):
                    row_max(1, 1, p)
                    if p == 0:
                        max_copy(0, 0)
                max_high(1, 1)
                max_low(1, 1)
                xn(3, 3)
                v_copy(2, 2)
                xn(4, 4)

                def step(n, r, end=NT):
                    mid = not isinstance(n, int)
                    at = lambda k: (r + k) % NBUF
                    for p in range(8):
                        if mid or n + 2 < end:
                            row_max(n + 2, at(2), p)
                        if p == 1 and (mid or n + 1 < end):
                            max_copy(n + 1, at(1))
                        if p == 2 and (mid or n >= 2):
                            ctx_recip(n - 2, at(-2))
                            ctx_div(n - 2, at(-2))
                        if p == 3 and (mid or n + 5 < end):
                            xn(n + 5, at(5))
                        if p == 4 and (mid or n + 3 < end):
                            v_copy(n + 3, at(3))
                        if p == 5 and (mid or n >= 2):
                            z_add(n - 2)
                    if mid or n >= 2:
                        z_stats(n - 2)
                    if mid or n + 2 < end:
                        max_high(n + 2, at(2))
                        max_low(n + 2, at(2))
                for n in range(NBUF):
                    step(n, n)
                with dve.Fori(1, NT // NBUF - 2) as i:
                    for r in range(NBUF):
                        step(NBUF * i + r, r)
                for n in range(NT - 2 * NBUF, NT):
                    step(n, n % NBUF)
                for t in (NT - 2, NT - 1):
                    ctx_recip(t, t % NBUF)
                    ctx_div(t, t % NBUF)
                    z_add(t)
                    z_stats(t)
                for t in range(NT):
                    dve.wait_ge(a_zs, t + 1)
                    dve.bn_aggr(mvz[:, t, :], statz[:, t, :]).then_inc(a_za, 1)
                dve.wait_ge(a_za, NT)
                dve.tensor_scalar(rstdz[:], mvz[:, :, 1], LN_EPS, None, ALU.add).then_inc(a_zve, 1)
                dve.wait_ge(a_zsd, 1)
                dve.reciprocal(rstdz[:], rstdz[:]).then_inc(a_zrs, 1)
                dve.wait_ge(a_zrs, 1)
                dve.wait_ge(a_xb, NT)
                for t in range(NT):
                    z = z_sb[:, t * P:(t + 1) * P]
                    dve.scalar_tensor_tensor(out=z, in0=z, scalar=mvz[:, t, 0:1], in1=gamma_sb[:],
                                             op0=ALU.subtract, op1=ALU.mult).then_inc(a_fin1, 1)
                for t in range(NT):
                    z = z_sb[:, t * P:(t + 1) * P]
                    dve.wait_ge(a_fin1, t + 1)
                    dve.scalar_tensor_tensor(out=x_sb[:, t, :], in0=z, scalar=rstdz[:, t:t + 1], in1=x_sb[:, t, :],
                                             op0=ALU.mult, op1=ALU.add).then_inc(a_fin, 1)
                dve.wait_ge(a_fin, NT)

            dve.wait_ge(s_x, 16)
            dve.wait_ge(s_rwp, 1)
            dve.tensor_copy(rwT[:], bank[0][:, 0:E]).then_inc(s_rws, 1)
            ffn(ffns[0])
            attention()
            ffn(ffns[1])

        @block.scalar
        def _(act):
            def ffn(f):
                wait(act, f.ve, 1)
                act.activation(rstd[:], rstd[:], ACT.Sqrt).then_inc(f.sd.sem, 1)

                def route(g, r):
                    wait(act, f.xtp, g + 1)
                    wait(act, f.lg, g - 1)
                    act.activation(xT_r[r], bank[r][:], ACT.Copy).then_inc(f.xts.sem, 1)
                    act.activation(xT_all[:, bass.ds(g * (GT * P), GT * P)], bank[r][:], ACT.Copy).then_inc(f.xts.sem, 1)
                    wait(act, f.d, GT * (g + 1))
                    wait(act, f.w, g - 1)
                    act.activation(e_r[r], d_r[r], ACT.Exp).then_inc(f.ex.sem, 1)
                route(0, 0)
                route(1, 1)
                with act.Fori(1, NG // 2) as i:
                    for r in range(2):
                        route(2 * i + r, r)
                for b in range(4):
                    wait(act, f.ktp, b + 1)
                    act.activation(KT[:, b * 512:(b + 1) * 512], bank[4 + b][:], ACT.Copy).then_inc(f.kts.sem, 1)

                def shared_up(g, r):
                    wait(act, f.shp, g + 1)
                    wait(act, f.shh, g - 1)
                    act.activation(shs[r][0:F, :], bank[r][0:F, :], ACT.Silu).then_inc(f.shs.sem, 1)
                    act.activation(shu[r][0:F, :], bank[2 + r][0:F, :], ACT.Copy).then_inc(f.shc.sem, 1)

                def shared_out(g, r):
                    wait(act, f.sho, g + 1)
                    wait(act, f.shx, g - 1)
                    act.activation(shy[r], bank[4 + r][:], ACT.Copy, scale=0.5).then_inc(f.shy.sem, 1)
                shared_up(0, 0)
                shared_up(1, 1)
                shared_out(0, 0)
                with act.Fori(1, NG // 2) as i:
                    for r in range(2):
                        shared_up(2 * i + r, r)
                        shared_out(2 * i + (r - 1), 1 - r)
                shared_out(NG - 1, 1)

                for q in range(NP2 // 2):
                    r = q % 2
                    wait(act, f.gtp, q + 1)
                    wait(act, f.gu, q - 1)
                    act.activation(gT[r], bank[r][:, 0:2 * P], ACT.Copy).then_inc(f.gts.sem, 1)
                    wait(act, f.gu, q + 1)
                    wait(act, f.hid, q - 1)
                    act.activation(sil[r][0:F, :], bank[2 + r][0:F, 0:4 * C], ACT.Silu).then_inc(f.sil.sem, 1)

            def attention():
                act.wait_ge(a_ve, 1)
                act.activation(rstd[:], rstd[:], ACT.Sqrt).then_inc(a_sd, 1)

                def xT_copy(t, r):
                    act.wait_ge(a_use, use("x", t) + 1)
                    act.activation(xTt_r[r % 2], bank[7][:, 0:P], ACT.Copy).then_inc(a_read, 1)

                def qk_copy(t, r):
                    act.wait_ge(a_use, use("q", t) + 1)
                    wait(act, a_parts, t - 1)
                    for i in range(2):
                        ins = act.activation(qk_r[r % 2][:, i * P:(i + 1) * P].rearrange("p (s g) -> p g s", g=NH),
                                             bank[7][:, i * P:(i + 1) * P].rearrange("p (g s) -> p g s", g=NH),
                                             ACT.Identity, bias=bqk_sb[:, i:i + 1])
                    ins.then_inc(a_read, 1)

                def ctx_copy(t, r):
                    act.wait_ge(a_PV, 4 * t + 4)
                    if not isinstance(t, int) or t >= 2:
                        act.wait_ge(a_cd[r % 2], lap(t - 2, r % 2, 2, 16 * 2))
                    act.activation(ctx_r[r % 2], bank[6][:, :], ACT.Copy).then_inc(a_cx, 1)

                def step(n, r, end=NT):
                    mid = not isinstance(n, int)
                    for tau in range(16):
                        kt, g = tau // 4, tau % 4
                        act.wait_ge(a_ST, 16 * n + (tau + 1))
                        if g == 0:
                            wait(act, a_PV, 4 * n + (kt - 1))
                        act.activation(p_r[tau % NPB], bank[4 + tau % 2][:, :], ACT.Exp, scale=SCALE).then_inc(a_P, 1)
                        if tau == 1 and (mid or n + 4 < end):
                            xT_copy(n + 4, r)
                        if tau == 5 and (mid or n >= 1):
                            ctx_copy(n - 1, (r - 1) % NBUF)
                        if tau == 7 and (mid or n + 4 < end):
                            qk_copy(n + 4, r)
                for t in range(NBUF):
                    xT_copy(t, t)
                    qk_copy(t, t)
                for n in range(NBUF):
                    step(n, n)
                with act.Fori(1, NT // NBUF - 1) as i:
                    for r in range(NBUF):
                        step(NBUF * i + r, r)
                for n in range(NT - NBUF, NT):
                    step(n, n % NBUF)
                ctx_copy(NT - 1, (NT - 1) % NBUF)
                act.wait_ge(a_zve, 1)
                act.activation(rstdz[:], rstdz[:], ACT.Sqrt).then_inc(a_zsd, 1)

            ffn(ffns[0])
            attention()
            ffn(ffns[1])

        @block.tensor
        def _(pe):
            def ffn(f):
                def route(g, r):
                    wait(pe, f.xn, g + 1)
                    wait(pe, f.xts, 2 * (g - 1))
                    for j in range(GT):
                        ins = pe.transpose(bank[r][:, j * P:(j + 1) * P], xn_sb[:, r, j, :], ident[:])
                    ins.then_inc(f.xtp.sem, 1)
                    wait(pe, f.xts, 2 * g + 1)
                    wait(pe, f.d, GT * (g - 1))
                    for j in range(GT):
                        ins = pe.matmul(bank[2 + r][:, j * E:(j + 1) * E], xT_r[r][:, j * P:(j + 1) * P], rwT[:],
                                        start=True, stop=True)
                    ins.then_inc(f.lg.sem, 1)
                route(0, 0)
                route(1, 1)
                with pe.Fori(1, NG // 2) as i:
                    for r in range(2):
                        route(2 * i + r, r)

                wait(pe, f.key, NG)
                for u in range(NT // 2):
                    ins = pe.transpose(bank[4 + u // 4][:, (u % 4) * P:(u % 4 + 1) * P], key[:, u * P:(u + 1) * P], ident[:])
                    if u % 4 == 3:
                        ins.then_inc(f.ktp.sem, 1)
                pe.wait_ge(s_wsh, 32)

                def up(g, r):
                    wait(pe, f.shc, g - 1)
                    pe.matmul(bank[r][0:F, :], wsgu_sb[:, 0:F], xT_all[:, bass.ds(g * (GT * P), GT * P)],
                              start=True, stop=True)
                    pe.matmul(bank[2 + r][0:F, :], wsgu_sb[:, F:2 * F], xT_all[:, bass.ds(g * (GT * P), GT * P)],
                              start=True, stop=True).then_inc(f.shp.sem, 1)

                def down(g, r):
                    wait(pe, f.shh, g + 1)
                    wait(pe, f.shy, g - 1)
                    for j in range(GT):
                        ins = pe.matmul(bank[4 + r][:, j * D:(j + 1) * D], shh[r][0:F, j * P:(j + 1) * P], wsd_sb[:],
                                        start=True, stop=True)
                    ins.then_inc(f.sho.sem, 1)

                wait(pe, f.xts, 2 * NG)
                wait(pe, f.kts, 4)
                up(0, 0)
                up(1, 1)
                down(0, 0)
                with pe.Fori(1, NG // 2) as i:
                    up(2 * i, 0)
                    down(2 * i - 1, 1)
                    up(2 * i + 1, 1)
                    down(2 * i, 0)
                down(NG - 1, 1)
                wait(pe, f.rnd, 32)
                pe.transpose(bank[6][0:C, 0:E], slots[0:E, :], ident[0:E, 0:E]).then_inc(f.slp.sem, 1)

                pe.wait_ge(s_wexp, 48)

                def slots_t(q):
                    r = q % 2
                    wait(pe, f.gts, q - 1)
                    for j in range(2):
                        k = 2 * q + j
                        wait(pe, f.gat[k % NGB], 16 * (k // NGB + 1))
                        ins = pe.transpose(bank[r][:, j * P:(j + 1) * P], gat[k % NGB][:, 0:D], ident[:])
                    ins.then_inc(f.gtp.sem, 1)

                def down_e(q):
                    r = q % 2
                    wait(pe, f.hid, q + 1)
                    wait(pe, f.ys, 4 * (q - 1))
                    for j in range(2):
                        for half in range(2):
                            e = 4 * q + 2 * j + half
                            rows = slice(half * C, (half + 1) * C)
                            ins = pe.matmul(bank[4 + r][rows, j * D:(j + 1) * D],
                                            hid[r][0:F, (2 * j + half) * C:(2 * j + half + 1) * C], wd_sb[:, e, :],
                                            start=True, stop=True)
                    ins.then_inc(f.y.sem, 1)

                wait(pe, f.shc, NG)
                wait(pe, f.shy, NG)
                slots_t(0)
                for q in range(NP2 // 2):
                    r = q % 2
                    wait(pe, f.gts, q + 1)
                    wait(pe, f.hid, q - 1)
                    for w, off in ((wg_sb, 0), (wu_sb, 4 * C)):
                        for m in range(4):
                            ins = pe.matmul(bank[2 + r][0:F, off + m * C:off + (m + 1) * C], w[:, 4 * q + m, :],
                                            gT[r][:, m * C:(m + 1) * C], start=True, stop=True)
                    ins.then_inc(f.gu.sem, 1)
                    if q + 1 < NP2 // 2:
                        slots_t(q + 1)
                    if q:
                        down_e(q - 1)
                down_e(NP2 // 2 - 1)

            pe.wait_ge(s_cst, 2)
            pe.wait_ge(s_wr, 16)
            pe.transpose(bank[0][:, 0:E], rw_sb[:], ident[0:E, 0:E]).then_inc(s_rwp, 1)
            pe.wait_ge(s_rws, 1)
            def attention():
                def misc(kind, t):
                    i = use(kind, t)
                    wait(pe, a_read, i)

                def xT(t, r):
                    pe.wait_ge(a_xn, t + 1)
                    misc("x", t)
                    pe.transpose(bank[7][:, 0:P], xn_r[r % 2], ident[:]).then_inc(a_use, 1)

                def qk(t, r):
                    misc("q", t)
                    for i in range(2):
                        ins = pe.matmul(bank[7][:, i * P:(i + 1) * P], wqk_sb[:, i * D:(i + 1) * D], xTt_r[r % 2],
                                        start=True, stop=True)
                    ins.then_inc(a_use, 1)

                def v(t, r):
                    misc("v", t)
                    for g in range(NH):
                        for jj in range(4):
                            ins = pe.matmul(bank[7][jj * 32:(jj + 1) * 32, g * 32:(g + 1) * 32],
                                            xTt_r[r % 2][:, g * HS:(g + 1) * HS],
                                            wv_sb[:].rearrange("e (k jj d) -> e jj k d", k=4, jj=4)[:, jj, :, :],
                                            start=True, stop=True, tile_position=(0, jj * 32))
                    ins.then_inc(a_use, 1)

                def maxT(t, r):
                    pe.wait_ge(a_hl, t + 1)
                    misc("m", t)
                    for g in range(NH):
                        ins = pe.transpose(bank[7][0:8, g * P // 2:(g + 1) * P // 2].bitcast(BF16),
                                           mhl_r[r % 2][:, 8 * g:8 * g + 8], identb[:])
                    ins.then_inc(a_use, 1)

                def proj(t, r):
                    pe.wait_ge(a_ct, t + 1)
                    misc("o", t)
                    pe.matmul(bank[7][:, 0:D], cT_r[r % 2], wo_sb[:], start=True, stop=True).then_inc(a_use, 1)

                def scores(t, r, tau):
                    g, qt = tau // 4, tau % 4
                    if tau == 0:
                        pe.wait_ge(a_stk[r], lap(t, r, NBUF, 16 * (NPART + 1)))
                    if tau % 2 == 0:
                        wait(pe, a_mx, 8 * t + (tau // 2 - 1))
                    rows = slice(0, MR)
                    ins = pe.matmul(bank[tau % 4][:, :], heads(q_st[r], rows, g)[:, qt * P:(qt + 1) * P],
                                    heads(k_st[r], rows, g), start=True, stop=True)
                    if tau % 2:
                        ins.then_inc(a_S, 1)

                def scores_t(t, r, tau):
                    kt, g = tau // 4, tau % 4
                    if tau == 0:
                        pe.wait_ge(a_mrow[r], lap(t, r, NBUF, 16))
                    wait(pe, a_P, 16 * t + (tau - 1))
                    rows = slice(0, P)
                    keys = heads(k_st[r], rows, g)[:, kt * P:(kt + 1) * P]
                    pe.matmul(bank[4 + tau % 2][:, :], keys, heads(q_st[r], rows, g), start=True, stop=True)\
                      .then_inc(a_ST, 1)

                def pv(t, r, kt):
                    pe.wait_ge(a_P, 16 * t + (4 * kt + 4))
                    if kt == 0:
                        wait(pe, a_cx, t)
                        pe.wait_ge(a_read, use("v", t) + 1)
                    for g in range(NH):
                        ins = pe.matmul(bank[6][32 * g:32 * g + 32, :], v_r[r][:, g, kt, :], p_r[(4 * kt + g) % NPB],
                                        start=(kt == 0), stop=(kt == 3), tile_position=(0, 32 * g))
                    ins.then_inc(a_PV, 1)

                def step(n, r, end=NT):
                    mid = not isinstance(n, int)
                    at = lambda k: (r + k) % NBUF
                    for tau in range(16):
                        if tau == 0 and (mid or n + 4 < end):
                            xT(n + 4, r)
                        if tau == 3 and (mid or n + 1 < end):
                            maxT(n + 1, at(1))
                        if tau == 6 and (mid or n + 4 < end):
                            qk(n + 4, r)
                        if tau == 9 and (mid or n + 3 < end):
                            v(n + 3, at(3))
                        if tau == 12 and (mid or n >= 2):
                            proj(n - 2, at(-2))
                        scores_t(n, r, tau)
                        if mid or n + 2 < end:
                            scores(n + 2, at(2), tau)
                        if tau == 3 and (mid or n >= 1):
                            pv(n - 1, at(-1), 3)
                        if tau % 4 == 3 and tau > 3:
                            pv(n, r, tau // 4 - 1)

                pe.wait_ge(s_wqk, 2)
                wait(pe, ffns[0].acca, NG)

                def prep(t):
                    xT(t, t)
                    qk(t, t)
                    if t < 3:
                        v(t, t)
                prep(0)
                for tau in range(16):
                    scores(0, 0, tau)
                prep(1)
                for tau in range(16):
                    scores(1, 1, tau)
                    if tau == 1:
                        maxT(0, 0)
                prep(2)
                prep(3)
                for n in range(NBUF):
                    step(n, n)
                with pe.Fori(1, NT // NBUF - 1) as i:
                    for r in range(NBUF):
                        step(NBUF * i + r, r)
                for n in range(NT - NBUF, NT):
                    step(n, n % NBUF)
                pv(NT - 1, (NT - 1) % NBUF, 3)
                for t in (NT - 2, NT - 1):
                    proj(t, t % NBUF)

            ffn(ffns[0])
            attention()
            ffn(ffns[1])



_INS = ["L0_attn_x", "L0_attn_wq", "L0_attn_bq", "L0_attn_wk", "L0_attn_bk", "L0_attn_wv", "L0_attn_bv", "L0_attn_wo",
        "L0_attn_bo", "L0_attn_gamma", "L0_attn_beta", "L0_ffn_router_w", "L0_ffn_w_gate", "L0_ffn_w_up",
        "L0_ffn_w_down", "L0_ffn_ws_gate_up", "L0_ffn_ws_down"]


def kernel(**inputs):
    import numpy as np
    import concourse.bacc as bacc
    from concourse.bass_utils import run_bass_kernel_spmd

    nc = bacc.Bacc("TRN2", target_bir_lowering=False, num_devices=1)
    arrays, args = {}, []
    for name in _INS:
        a = np.ascontiguousarray(inputs[name])
        arrays[f"in_{name}"] = a
        args.append(nc.dram_tensor(f"in_{name}", a.shape, mybir.dt.from_np(a.dtype), kind="ExternalInput").ap())
    out = nc.dram_tensor("out_x", inputs["L0_attn_x"].shape, F32, kind="ExternalOutput").ap()
    macaron_kernel(nc, *args, out)
    r = run_bass_kernel_spmd(nc, [arrays], core_ids=[0])
    return r.results[0]["out_x"]
```

```python
from contextlib import ExitStack

import concourse.bass as bass
from concourse import mybir

F32 = mybir.dt.float32
BF16 = mybir.dt.bfloat16
U32 = mybir.dt.uint32
ALU = mybir.AluOpType
ACT = mybir.ActivationFunctionType
X = mybir.AxisListType.X
P = 128


def macaron_kernel(nc, x_in, wq, bq, wk, bk, wv, bv, wo, bo, gamma, beta,
                   router_w, w_gate, w_up, w_down, ws_gate_up, ws_down, out):
    B, S, D = x_in.shape
    T = B * S
    NT = T // P
    E, _, F = w_gate.shape
    K8, C = 8, 64
    NP2 = E // 2
    GT = 4
    NG = NT // GT
    NACC = 4
    ACC = T + C
    XW = D + E
    H, HD = 16, 8
    HS = S // H
    NH = P // HS
    NPART = 3
    NR = NPART * NPART * HD
    MR = P - 2
    SCALE = float(HD) ** -0.5
    LN_EPS = 1e-5
    NBUF = 4
    NPB = 8
    AW = 19072
    assert 2 * NACC == NPB and NH * HS == P and C * 2 == P and T % (P * GT) == 0

    x_rows = x_in.rearrange("b s d -> (b s) d")
    out_rows = out.rearrange("b s d -> (b s) d")
    xw_dram = [nc.dram_tensor(f"dispatch_rows{p}", [T, XW], F32, kind="Internal").ap() for p in range(2)]
    parts_dram = nc.dram_tensor("qk_parts", [4, 2 * NPART, P, P], BF16, kind="Internal").ap()
    ctx_dram = nc.dram_tensor("ctx", [4, P, 512], F32, kind="Internal").ap()
    acc_dram = [nc.dram_tensor(f"routed_sums{p}", [NACC * ACC, D], F32, kind="Internal").ap() for p in range(2)]

    with ExitStack() as ctx:
        def sb(name, shape, dt=F32):
            return ctx.enter_context(nc.sbuf_tensor(name, shape, dt))

        def sem(name):
            return ctx.enter_context(nc.semaphore(name))

        def wait(eng, s, value):
            if isinstance(s, Event):
                s, value = s.sem, value + s.base
            if isinstance(value, int) and value <= 0:
                return
            eng.wait_ge(s, value)

        def wait_each(eng, *waits):
            ready, taken = [], []
            for s, value in waits:
                if isinstance(s, Event):
                    s, value = s.sem, value + s.base
                if not isinstance(value, int):
                    count = eng.alloc_register()
                    eng.reg_mov(count, value)
                    taken.append(count)
                    value = count
                elif value <= 0:
                    continue
                ready.append((s, value))
            for s, value in ready:
                eng.wait_ge(s, value)
            for count in taken:
                eng.free_register(count)

        def wait_apart(eng, *waits):
            wait_each(eng, (s_cst, 1), *waits)

        x_sb = sb("x_sb", [P, NT, D])
        z_sb = sb("z_sb", [P, NT * D])
        xT_all = z_sb[:]
        wg_sb = sb("wg_sb", [P, E, F])
        wu_sb = sb("wu_sb", [P, E, F])
        wd_sb = sb("wd_sb", [F, E, D])
        wsgu_sb = sb("wsgu_sb", [P, 2 * F])
        wsd_sb = sb("wsd_sb", [F, D])
        rw_sb = sb("rw_sb", [E, D])
        rwT = sb("rwT", [P, E])
        ident = sb("ident", [P, P])
        identb = sb("identb", [P, P], BF16)
        zeros = sb("zeros", [P, 10 * D])
        keyt = sb("keyt", [P, NT])
        slot_c = sb("slot_c", [P, 1])
        acc_off = sb("acc_off", [P, NP2])
        stats = sb("stats", [P, NT, 6])
        mv = sb("mv", [P, NT, 2])
        rstd = sb("rstd", [P, NT])
        xn_sb = sb("xn_sb", [P, 2, GT, D])
        arena = sb("arena", [P, AW])

        used = [0]

        def carve(words, start=None):
            if start is not None:
                used[0] = start
            a = used[0]
            used[0] += words
            assert used[0] <= AW, used[0]
            return arena[:, a:a + words]

        xT_r = [carve(GT * P) for _ in range(2)]
        d_r = [carve(GT * E) for _ in range(2)]
        e_r = [carve(GT * E) for _ in range(2)]
        top_r = [carve(GT * K8) for _ in range(2)]
        w_r = [carve(GT * E) for _ in range(2)]
        m_r = [carve(GT) for _ in range(2)]
        den_r = [carve(GT) for _ in range(2)]
        key = carve(NT * E)
        KT = carve(NT * E)
        cand = carve(C)
        merged = carve(2 * C)
        slots = carve(C)
        kc = carve(NP2)
        tokf = carve(NP2)
        emp = carve(NP2)
        gidx = carve(NP2).bitcast(U32)
        sidx = carve(NP2).bitcast(U32)
        NGB = 16
        gat = [carve(XW) for _ in range(NGB)]
        gT = [carve(2 * P) for _ in range(2)]
        sil = [carve(4 * C) for _ in range(2)]
        hid = [carve(4 * C) for _ in range(2)]
        NYB = 4
        y_r = [carve(D) for _ in range(NYB)]
        shh = [carve(GT * P) for _ in range(2)]

        QC = H * P
        q_st = [carve(QC // 2, 0 if i == 0 else None).bitcast(BF16) for i in range(NBUF)]
        k_st = [carve(QC // 2).bitcast(BF16) for i in range(NBUF)]
        p_r = [carve(H * HS) for _ in range(NPB)]
        v_all = carve(NBUF * NH * 4 * 32)
        v_r = [v_all[:, i * NH * 128:(i + 1) * NH * 128].rearrange("p (g k c) -> p g k c", g=NH, k=4) for i in range(NBUF)]
        acc_r = p_r
        shs = [xT_r[0], xT_r[1]]
        shu = [acc_r[0], acc_r[1]]
        shy = [acc_r[2], acc_r[3]]
        xn_r = [carve(P) for _ in range(2)]
        xTt_r = [carve(P) for _ in range(2)]
        qk_r = [carve(2 * P) for _ in range(2)]
        res_r = [carve(2 * P) for _ in range(2)]
        part_r = [carve(3 * P).bitcast(BF16) for _ in range(2)]
        ctx_r = [carve(H * HS) for _ in range(2)]
        num_r = [carve(P) for _ in range(2)]
        den2_r = [carve(P) for _ in range(2)]
        cT_r = [carve(P) for _ in range(2)]
        mx_r = [carve(NH * 4) for _ in range(2)]
        mhl_r = [carve(NH * 4).bitcast(BF16) for _ in range(2)]
        mT_r = [carve(2 * P).bitcast(BF16)[0:8, :] for _ in range(2)]

        def heads(stack, rows, g):
            return stack[rows, :].rearrange("r (c g) -> r c g", g=NH)[:, :, g]

        wqk_raw = sb("wqk_raw", [P, 2 * D])
        wqk_sb = sb("wqk_sb", [P, 2 * D])
        wv_sb = sb("wv_sb", [P, D])
        wo_sb = sb("wo_sb", [P, D])
        bqk_sb = sb("bqk_sb", [P, 2])
        bv_sb = sb("bv_sb", [P, 32])
        bo_sb = sb("bo_sb", [P, D])
        gamma_sb = sb("gamma_sb", [P, D])
        beta_sb = sb("beta_sb", [P, D])
        statz = sb("statz", [P, NT, 6])
        mvz = sb("mvz", [P, NT, 2])
        rstdz = sb("rstdz", [P, NT])
        negm = sb("negm", [P, NT])

        psum = ctx.enter_context(nc.psum_tensor("psum", [P, 8 * 512], F32))
        bank = [psum[:, i * 512:(i + 1) * 512] for i in range(8)]

        s_x = [sem(f"x_loaded{c}") for c in range(4)]
        s_wr = sem("router_loaded")
        s_wsh = sem("shared_loaded")
        s_wexp = sem("experts_loaded")
        s_cst = sem("constants_ready")
        s_cst1 = sem("constants_step")
        s_zero = sem("zeros_ready")
        s_rwp = sem("router_transposed")
        s_rws = sem("router_copied")
        s_acc0 = [sem(f"sums_zeroed{p}") for p in range(2)]
        s_out = sem("out_stored")

        totals = dict(stats_done=NT, var_ready=NT, eps_added=1, std_ready=1, rstd_ready=1,
                      xn_ready=NG, xT_in_psum=NG, xT_copied=2 * NG, logits_in_psum=NG, row_max=NG, shifted_logits=NT,
                      top8_found=NT, top8_marked=NT, keys_ready=NG, exp_ready=NG, masked_exp=NG, exp_sum=NG,
                      exp_recip=NG, weights_ready=NG, keys_transposed=4, keys_copied=4, list_step=38,
                      slots_transposed=1, indices_ready=1, shared_up_in_psum=NG, shared_up_copied=NG, shared_silu=NG, shared_hidden=NG,
                      shared_out_in_psum=NG, shared_out_copied=NG, shared_added=NG, x_centered=NG, slotsT_in_psum=NP2 // 2, slotsT_copied=NP2 // 2,
                      gate_up_in_psum=NP2 // 2, silu_ready=NP2 // 2, hidden_ready=NP2 // 2, y_in_psum=NP2 // 2,
                      y_weighted=2 * NP2, sums_step=2 * NG, sums_paired=NG, sums_added=NG)
        for i in range(2):
            totals[f"xn_stored{i}"] = totals[f"weights_stored{i}"] = 16 * NG // 2
            totals[f"scattered{i}"] = 16 * NP2 // 2
            totals[f"sums_loaded{i}"] = 16 * NACC * NG // 2
        for i in range(NGB):
            totals[f"gathered{i}"] = 16 * NP2 // NGB
        ffn_sems = {name: sem(name) for name in totals}

        class Event:

            def __init__(self, name, p):
                self.sem, self.base = ffn_sems[name], p * totals[name]

        class Ffn:

            def __init__(self, p):
                n = lambda s: Event(s, p)
                self.p = p
                self.stat, self.aggr, self.sd, self.rs = n("stats_done"), n("var_ready"), n("std_ready"), n("rstd_ready")
                self.ve = n("eps_added")
                self.xn, self.xtp, self.xts = n("xn_ready"), n("xT_in_psum"), n("xT_copied")
                self.lg, self.mx, self.d = n("logits_in_psum"), n("row_max"), n("shifted_logits")
                self.top, self.rep, self.key = n("top8_found"), n("top8_marked"), n("keys_ready")
                self.ex, self.es, self.den = n("exp_ready"), n("masked_exp"), n("exp_sum")
                self.rden, self.w = n("exp_recip"), n("weights_ready")
                self.cen = n("x_centered")
                self.xns = [n(f"xn_stored{i}") for i in range(2)]
                self.ws = [n(f"weights_stored{i}") for i in range(2)]
                self.ktp, self.kts = n("keys_transposed"), n("keys_copied")
                self.rnd = n("list_step")
                self.slp = n("slots_transposed")
                self.idx = n("indices_ready")
                self.shp, self.shs, self.shh = n("shared_up_in_psum"), n("shared_silu"), n("shared_hidden")
                self.shc = n("shared_up_copied")
                self.sho, self.shy, self.shx = n("shared_out_in_psum"), n("shared_out_copied"), n("shared_added")
                self.gat = [n(f"gathered{i}") for i in range(NGB)]
                self.gtp, self.gts = n("slotsT_in_psum"), n("slotsT_copied")
                self.gu, self.sil, self.hid = n("gate_up_in_psum"), n("silu_ready"), n("hidden_ready")
                self.y, self.ys = n("y_in_psum"), n("y_weighted")
                self.sca = [n(f"scattered{i}") for i in range(2)]
                self.accl = [n(f"sums_loaded{i}") for i in range(2)]
                self.pair = n("sums_paired")
                self.add, self.acca = n("sums_step"), n("sums_added")

        ffns = [Ffn(0), Ffn(1)]
        s_watt = sem("att_weights_loaded")
        s_wqk = sem("wqk_permuted")
        s_vini = sem("v_ring_filled")
        s_kini = sem("k_stacks_filled")
        s_vst = sem("v_ring_step")
        a_xc = sem("a_x_centered")
        a_stat, a_aggr, a_ve, a_sd, a_rs = sem("a_stats"), sem("a_var"), sem("a_eps"), sem("a_std"), sem("a_rstd")
        a_xn = sem("a_xn_ready")
        a_zb = sem("a_residual_ready")
        a_xb = sem("a_x_plus_beta")
        a_use = sem("a_misc_written")
        a_read = sem("a_misc_read")
        a_part1, a_res1, a_part2, a_parts = sem("a_part1"), sem("a_rest1"), sem("a_part2"), sem("a_parts_ready")
        a_stk = [sem(f"a_stack_loaded{i}") for i in range(NBUF)]
        a_mrow = [sem(f"a_max_rows_loaded{i}") for i in range(NBUF)]
        a_S, a_mx = sem("a_scores_in_psum"), sem("a_max_ready")
        a_pst, a_cst = sem("a_parts_stored"), sem("a_ctx_stored")
        a_hi, a_hl = sem("a_max_high"), sem("a_max_split")
        a_ST, a_P, a_PV = sem("a_scoresT_in_psum"), sem("a_exp_ready"), sem("a_pv_done")
        a_cx = sem("a_ctx_copied")
        a_cd = [sem(f"a_ctx_moved{i}") for i in range(2)]
        a_rc, a_ct = sem("a_recip"), sem("a_ctxT_ready")
        a_zs, a_za = sem("a_z_stats"), sem("a_z_var")
        a_zve, a_zsd, a_zrs = sem("a_z_eps"), sem("a_z_std"), sem("a_z_rstd")
        a_znm, a_zn = sem("a_z_neg_mean"), sem("a_z_normalised")
        a_fin1, a_fin = sem("a_final_scaled"), sem("a_final_added")

        uses = [("x", 0), ("q", 0), ("v", 0), ("x", 1), ("q", 1), ("v", 1), ("x", 2), ("q", 2), ("v", 2),
                ("x", 3), ("q", 3), ("m", 0)]
        for n in range(NT + 2):
            uses += [u for u in (("x", n + 4), ("m", n + 1), ("q", n + 4), ("v", n + 3), ("o", n - 2))
                     if 0 <= u[1] < NT]
        where = {u: i for i, u in enumerate(uses)}

        def use(kind, t):
            if isinstance(t, int):
                return where[kind, t]
            return 5 * t + (where[kind, 10] - 50)

        def lap(n, r, ring, per):
            return n * (per // ring) + (per - r * (per // ring))

        block = ctx.enter_context(nc.Block())

        @block.sync
        def _(sp):
            for c in range(4):
                part = slice(c * NT // 4, (c + 1) * NT // 4)
                sp.dma_start(x_sb[:, part, :], x_rows.rearrange("(i p) d -> p i d", p=P)[:, part, :]).then_inc(s_x[c], 16)
            sp.dma_start(rw_sb[:], router_w).then_inc(s_wr, 16)
            sp.dma_start(wsgu_sb[:], ws_gate_up).then_inc(s_wsh, 16)
            sp.dma_start(wsd_sb[:], ws_down).then_inc(s_wsh, 16)
            sp.wait_ge(s_zero, 1)

            def zero_sums(p, part=0, parts=1):
                z = acc_dram[p].rearrange("(c p r) d -> c p (r d)", p=P, r=10)
                for c in range(part, z.shape[0], parts):
                    sp.dma_start(z[c], zeros[:]).then_inc(s_acc0[p], 16)

            sp.dma_start(wv_sb[:], wv).then_inc(s_watt, 16)
            sp.dma_start(wo_sb[:], wo.rearrange("(j d) n -> d j n", d=HD)).then_inc(s_watt, 16)
            for i, (w, b) in enumerate(((wq, bq), (wk, bk))):
                sp.dma_start(wqk_raw[:, i * D:(i + 1) * D], w).then_inc(s_watt, 16)
                sp.dma_start(bqk_sb[:, i:i + 1], b.rearrange("(j d o) -> d j o", d=HD, o=1), allow_slow_non_contiguous=True).then_inc(s_watt, 16)
            for jj in range(4):
                sp.dma_start(bv_sb[jj * 32:(jj + 1) * 32, :].rearrange("p (k d) -> p k d", k=4),
                             bv.rearrange("(o k jj d) -> jj o k d", o=1, k=4, jj=4)[jj].to_broadcast([32, 4, HD]))\
                  .then_inc(s_watt, 16)
            for t, b in ((bo_sb, bo), (gamma_sb, gamma), (beta_sb, beta)):
                sp.dma_start(t[:], b.rearrange("(o c) -> o c", o=1).to_broadcast([P, D])).then_inc(s_watt, 16)
            zero_sums(0, 0, 3)

            def ffn(f):
                rows = xw_dram[f.p].rearrange("(i p) c -> p i c", p=P)

                def store(g, r):
                    wait(sp, f.xn, g + 1)
                    sp.dma_start(rows[:, bass.ds(g * GT, GT), 0:D], xn_sb[:, r, :, :]).then_inc(f.xns[r].sem, 16)

                def store_w(g, r):
                    wait(sp, f.w, g + 1)
                    sp.dma_start(rows[:, bass.ds(g * GT, GT), D:XW], w_r[r].rearrange("p (i e) -> p i e", i=GT))\
                      .then_inc(f.ws[r].sem, 16)
                store(0, 0)
                store(1, 1)
                store_w(0, 0)
                if f.p == 0:
                    zero_sums(0, 1, 3)
                with sp.Fori(1, NG // 2) as i:
                    for r in range(2):
                        store(2 * i + r, r)
                        store_w(2 * i + (r - 1), 1 - r)
                store_w(NG - 1, 1)
                if f.p == 0:
                    zero_sums(0, 2, 3)
                    for w, t in ((w_gate, wg_sb), (w_up, wu_sb), (w_down, wd_sb)):
                        sp.dma_start(t[:], w.rearrange("e k n -> k e n")).then_inc(s_wexp, 16)
                wait(sp, f.shx, NG)
                wait(sp, f.sca[0], 16 * (NP2 // 2))
                wait(sp, f.sca[1], 16 * (NP2 // 2))
                accs = acc_dram[f.p].rearrange("(a t) d -> a t d", a=NACC)[:, 0:T, :].rearrange("a (i p) d -> a p i d", p=P)

                def load(g, r):
                    wait(sp, f.acca, g - 1)
                    for a in range(NACC):
                        sp.dma_start(acc_r[r * NACC + a].rearrange("p (i d) -> p i d", i=GT),
                                     accs[a, :, bass.ds(g * GT, GT), :]).then_inc(f.accl[r].sem, 16)
                def store_out(g):
                    wait(sp, f.acca, g + 1)
                    sp.dma_start(out_rows.rearrange("(i p) d -> p i d", p=P)[:, bass.ds(g * GT, GT), :],
                                 x_sb[:, bass.ds(g * GT, GT), :]).then_inc(s_out, 16)
                load(0, 0)
                load(1, 1)
                with sp.Fori(1, NG // 2) as i:
                    for r in range(2):
                        load(2 * i + r, r)
                        if f.p == 1:
                            store_out(2 * i + (r - 2))
                if f.p == 1:
                    store_out(NG - 2)
                    store_out(NG - 1)
                    sp.wait_ge(s_out, 16 * NG)

            def attention():
                def max_rows(t, r):
                    sp.wait_ge(a_read, use("m", t) + 1)
                    sp.dma_start(q_st[r][MR:P, :].rearrange("h (q c) -> h q c", q=4), mT_r[r % 2])\
                      .then_inc(a_mrow[r], 16)

                def stack_store(t, r):
                    sp.wait_ge(a_parts, t + 1)
                    sp.dma_start(parts_dram[r].rearrange("c p t -> p c t"),
                                 part_r[r % 2].rearrange("p (c t) -> p c t", t=P)).then_inc(a_pst, 16)

                def stack_load(t, r):
                    wait_each(sp, (a_ST, 16 * (t - 3)), (a_pst, 16 * t + 16))
                    parts = parts_dram[r].rearrange("c p t -> c (p t)")
                    for a in range(NPART):
                        rows = slice(a * NPART * HD, (a + 1) * NPART * HD)
                        sp.dma_start(q_st[r][rows, :], parts[a:a + 1].to_broadcast([NPART, P * P])).then_inc(a_stk[r], 16)
                    sp.dma_start(k_st[r][0:NR, :], parts[NPART:2 * NPART].rearrange("(o c) x -> o (c x)", o=1)
                                 .to_broadcast([NPART, NPART * P * P])).then_inc(a_stk[r], 16)

                def ctx_store(t, r):
                    sp.wait_ge(a_cx, t + 1)
                    sp.dma_start(ctx_dram[r], ctx_r[r % 2]).then_inc(a_cst, 16)

                def ctx_load(t, r):
                    wait_each(sp, (a_use, use("o", t - 2) + 1 if not isinstance(t, int) or t >= 2 else 0),
                              (a_cst, 16 * t + 16))
                    for k, dst in enumerate((num_r, den2_r)):
                        src = ctx_dram[r].rearrange("(g x) c -> g (x c)", g=NH)[:, k * HD * 512:(k + 1) * HD * 512]
                        sp.dma_start(dst[r % 2].rearrange("p (g s) -> p g s", g=NH),
                                     src.rearrange("g (p s) -> p g s", s=HS)).then_inc(a_cd[r % 2], 16)

                sp.wait_ge(s_vini, 2)
                sp.wait_ge(s_kini, 1)
                for t in range(3):
                    stack_store(t, t)
                    stack_load(t, t)
                stack_store(3, 3)
                max_rows(0, 0)
                def step(n, r, end=NT):
                    mid = not isinstance(n, int)
                    if mid or n + 3 < end:
                        stack_load(n + 3, (r + 3) % NBUF)
                    if mid or n + 1 < end:
                        max_rows(n + 1, (r + 1) % NBUF)
                    if mid or n >= 1:
                        ctx_store(n - 1, (r - 1) % NBUF)
                    if mid or n + 4 < end:
                        stack_store(n + 4, r)
                    if mid or n >= 1:
                        ctx_load(n - 1, (r - 1) % NBUF)
                for n in range(NBUF):
                    step(n, n)
                    zero_sums(1, n, NBUF)
                with sp.Fori(1, NT // NBUF - 1) as i:
                    for r in range(NBUF):
                        step(NBUF * i + r, r)
                for n in range(NT - NBUF, NT):
                    step(n, n % NBUF)
                ctx_store(NT - 1, (NT - 1) % NBUF)
                ctx_load(NT - 1, (NT - 1) % NBUF)

            ffn(ffns[0])
            attention()
            ffn(ffns[1])

        @block.gpsimd
        def _(pool):
            pool.memset(zeros[:], 0.0).then_inc(s_zero, 1)
            pool.memset(ident[:], 0.0).then_inc(s_cst1, 1)
            pool.memset(identb[:], 0.0).then_inc(s_cst1, 1)
            pool.wait_ge(s_cst1, 2)
            for t in (ident, identb):
                pool.affine_select(out=t[:], in_=t[:], compare_op=ALU.not_equal, fill=1.0, base=0,
                                   pattern=[[-1, P]], channel_multiplier=1).then_inc(s_cst, 1)
            f32 = dict(allow_small_or_imprecise_dtypes=True)
            pool.iota(keyt[:], pattern=[[-P, NT]], base=T, channel_multiplier=-1, **f32).then_inc(s_cst, 1)
            for half in range(2):
                rows = slice(half * C, (half + 1) * C)
                pool.wait_ge(s_cst, 3 + 2 * half)
                pool.iota(slot_c[rows, :], pattern=[[0, 1]], base=0, channel_multiplier=1, **f32).then_inc(s_cst, 1)
                pool.iota(acc_off[rows, :], pattern=[[0, NP2 // 2], [2 * ACC, 2]], base=half * ACC,
                          channel_multiplier=0, **f32).then_inc(s_cst, 1)

            def ffn(f):
                def normalise(g, r):
                    xn = xn_sb[:, r, :, :]
                    wait(pool, f.xns[r], 16 * ((g - r) // 2) if isinstance(g, int) else 8 * (g - r))
                    wait(pool, f.xtp, g - 1)
                    pool.tensor_tensor(xn, x_sb[:, bass.ds(g * GT, GT), :],
                                       mv[:, bass.ds(g * GT, GT), 0:1].to_broadcast([P, GT, D]),
                                       ALU.subtract).then_inc(f.cen.sem, 1)
                    wait(pool, f.cen, g + 1)
                    pool.tensor_tensor(xn, xn, rstd[:, bass.ds(g * GT, GT)].unsqueeze(2).to_broadcast([P, GT, D]),
                                       ALU.mult).then_inc(f.xn.sem, 1)
                pool.wait_ge(s_cst, 7)
                wait(pool, f.rs, 1)
                normalise(0, 0)
                normalise(1, 1)
                with pool.Fori(1, NG // 2) as i:
                    for r in range(2):
                        normalise(2 * i + r, r)

                def shared_mul(g, r):
                    wait(pool, f.shx, g - 1)
                    wait(pool, f.shs, g + 1)
                    wait(pool, f.shc, g + 1)
                    wait(pool, f.sho, g - 1)
                    pool.tensor_tensor(shh[r][0:F, :], shs[r][0:F, :], shu[r][0:F, :], ALU.mult).then_inc(f.shh.sem, 1)

                def shared_add(g, r):
                    wait(pool, f.shh, g + 2 if not isinstance(g, int) or g + 2 < NG else NG)
                    wait(pool, f.shy, g + 1)
                    xs = x_sb[:, bass.ds(g * GT, GT), :]
                    pool.tensor_tensor(xs, xs, shy[r].rearrange("p (i d) -> p i d", i=GT), ALU.add).then_inc(f.shx.sem, 1)
                shared_mul(0, 0)
                shared_mul(1, 1)
                shared_add(0, 0)
                with pool.Fori(1, NG // 2) as i:
                    for r in range(2):
                        shared_mul(2 * i + r, r)
                        shared_add(2 * i + (r - 1), 1 - r)
                shared_add(NG - 1, 1)

                wait(pool, f.shx, NG)
                wait(pool, f.idx, 1)
                for r in range(2):
                    wait(pool, f.xns[r], 16 * (NG // 2))
                    wait(pool, f.ws[r], 16 * (NG // 2))
                pool.wait_ge(s_acc0[f.p], 16 * (NACC * ACC // (P * 10)))

                def gather(k):
                    wait(pool, f.ys, 4 * ((k - NGB) // 2 + 1) if k >= NGB else 0)
                    pool.indirect_dma_start(out=gat[k % NGB], out_offset=None, in_=xw_dram[f.p],
                                            in_offset=bass.IndirectOffsetOnAxis(ap=gidx[:, k:k + 1], axis=0),
                                            ).then_inc(f.gat[k % NGB].sem, 16)

                LEAD = 12
                for k in range(LEAD):
                    gather(k)
                for k in range(NP2):
                    if k + LEAD < NP2:
                        gather(k + LEAD)
                    wait(pool, f.ys, 4 * (k // 2) + 2 * (k % 2) + 2)
                    wait(pool, f.sca[k % 2], 16 * (k // 2))
                    pool.indirect_dma_start(out=acc_dram[f.p], in_=y_r[k % NYB], in_offset=None,
                                            out_offset=bass.IndirectOffsetOnAxis(ap=sidx[:, k:k + 1], axis=0),
                                            compute_op=ALU.add).then_inc(f.sca[k % 2].sem, 16)

                def pair(g, r):
                    wait(pool, f.accl[r], 16 * NACC * ((g - r) // 2 + 1) if isinstance(g, int)
                                 else 8 * NACC * (g - r) + 16 * NACC)
                    a, b = acc_r[r * NACC + NACC - 2], acc_r[r * NACC + NACC - 1]
                    pool.tensor_tensor(a, a, b, ALU.add).then_inc(f.pair.sem, 1)
                if f.p == 1:
                    with pool.Fori(0, NG // 2) as i:
                        for r in range(2):
                            pair(2 * i + r, r)
                    return
                clear_stacks()
                pool.wait_ge(s_watt, 16 * 13)
                for g in range(NG):
                    pair(g, g % 2)
                    if g in (2, 4, 6):
                        center(g // 2 - 1, g // 2 - 1)
                    if g in (3, 5):
                        split(g // 2 - 1, g // 2 - 1)

            def clear_stacks():
                wait(pool, ffns[0].ys, 2 * NP2)
                for i in range(NBUF):
                    ins = pool.memset(q_st[i][:, :], 0.0)
                ins.then_inc(s_vini, 1)
                pool.memset(v_all, 0.0).then_inc(s_vst, 1)
                pool.wait_ge(s_vst, 1)
                pool.memset(v_all.rearrange("p (a c) -> p a c", c=32)[:, :, HD:2 * HD], 1.0).then_inc(s_vini, 1)
                pool.wait_ge(s_vini, 2)

            def center(t, r):
                xt = x_sb[:, bass.ds(t, 1), :].rearrange("p a d -> p (a d)")
                wait(pool, a_rs, 1 if isinstance(t, int) else 0)
                wait(pool, a_use, use("x", t - 2) + 1 if not isinstance(t, int) or t >= 2 else 0)
                pool.tensor_tensor(xn_r[r % 2], xt, mv[:, bass.ds(t, 1), 0].to_broadcast([P, D]), ALU.subtract)\
                    .then_inc(a_xc, 1)
                pool.wait_ge(a_xc, t + 1)
                pool.tensor_tensor(xn_r[r % 2], xn_r[r % 2], rstd[:, bass.ds(t, 1)].to_broadcast([P, D]), ALU.mult)\
                    .then_inc(a_xn, 1)
                pool.wait_ge(a_xn, t + 1)
                pool.tensor_tensor(z_sb[:, bass.ds(t * P, P)], xn_r[r % 2], bo_sb[:], ALU.add).then_inc(a_zb, 1)
                pool.tensor_tensor(xt, xt, beta_sb[:], ALU.add).then_inc(a_xb, 1)

            def split(t, r):
                p1, p2, p3 = [part_r[r % 2].rearrange("p (qk c t) -> p c qk t", qk=2, c=3)[:, c] for c in range(3)]
                qk, res = [b[r % 2].rearrange("p (qk t) -> p qk t", qk=2) for b in (qk_r, res_r)]
                waits = [(a_read, use("q", t) + 1)]
                if not isinstance(t, int) or t >= 2:
                    waits.append((a_pst, 16 * (t - 1)))
                wait_apart(pool, *waits)
                pool.tensor_copy(p1, qk).then_inc(a_part1, 1)
                pool.wait_ge(a_part1, t + 1)
                pool.tensor_tensor(res, qk, p1, ALU.subtract).then_inc(a_res1, 1)
                wait_apart(pool, (a_res1, t + 1))
                pool.tensor_copy(p2, res).then_inc(a_part2, 1)
                pool.wait_ge(a_part2, t + 1)
                pool.tensor_tensor(p3, res, p2, ALU.subtract).then_inc(a_parts, 1)

            def attention():
                def prep(t, r):
                    center(t, r)
                    split(t, r)
                split(2, 2)
                wait(pool, a_rs, 2)
                for t in range(3, 2 * NBUF):
                    prep(t, t % NBUF)
                with pool.Fori(2, NT // NBUF) as i:
                    for r in range(NBUF):
                        prep(NBUF * i + r, r)
                for g in range(NG):
                    z = z_sb[:, g * GT * P:(g + 1) * GT * P].rearrange("p (i d) -> p i d", i=GT)
                    pool.wait_ge(a_zn, GT * (g + 1))
                    pool.tensor_tensor(z, z, gamma_sb[:].unsqueeze(1).to_broadcast([P, GT, P]), ALU.mult).then_inc(a_fin1, 1)

            ffn(ffns[0])
            attention()
            ffn(ffns[1])

        @block.vector
        def _(dve):
            def variance(first, last, stat, aggr, ve):
                inc = lambda ins, s: ins.then_inc(s.sem if isinstance(s, Event) else s, 1)
                for i in range(first, last):
                    wait(dve, stat, i + 1)
                    inc(dve.bn_aggr(mv[:, i, :], stats[:, i, :]), aggr)
                wait(dve, aggr, last)
                inc(dve.tensor_scalar(rstd[:, first:last], mv[:, first:last, 1], LN_EPS, None, ALU.add), ve)

            def inverse_std(first, last, count, sd, rs):
                wait(dve, sd, count)
                dve.reciprocal(rstd[:, first:last], rstd[:, first:last])\
                   .then_inc(rs.sem if isinstance(rs, Event) else rs, 1)
                wait(dve, rs, count)

            def v_copy(t, r):
                dve.wait_ge(a_use, use("v", t) + 1)
                wait(dve, a_PV, 4 * (t - 3))
                b = bv_sb[:].rearrange("p (k c) -> p k c", k=4).unsqueeze(1).to_broadcast([P, NH, 4, HD])
                dve.tensor_tensor(v_r[r][:, :, :, 0:HD], bank[7][:, 0:P].rearrange("p (g k c) -> p g k c", g=NH, k=4),
                                  b, ALU.add).then_inc(a_read, 1)

            def ffn(f):
                variance(0, NT, f.stat, f.aggr, f.ve)
                inverse_std(0, NT, 1, f.sd, f.rs)

                def route(g, r):
                    lg = bank[2 + r][:, 0:GT * E].rearrange("p (j e) -> p j e", j=GT)
                    d = d_r[r].rearrange("p (j e) -> p j e", j=GT)
                    e = e_r[r].rearrange("p (j e) -> p j e", j=GT)
                    top = top_r[r].rearrange("p (j e) -> p j e", j=GT)
                    kk = key.rearrange("p (i e) -> p i e", e=E)
                    wait(dve, f.lg, g + 1)
                    dve.tensor_reduce(m_r[r], lg, X, ALU.max).then_inc(f.mx.sem, 1)
                    wait(dve, f.mx, g + 1)
                    for j in range(GT):
                        dve.tensor_scalar(d[:, j, :], lg[:, j, :], m_r[r][:, j:j + 1], -88.0,
                                          ALU.subtract, ALU.max).then_inc(f.d.sem, 1)
                    for j in range(GT):
                        wait_apart(dve, (f.d, g * GT + j + 1))
                        dve.max(top[:, j, :], d[:, j, :]).then_inc(f.top.sem, 1)
                    for j in range(GT):
                        wait_apart(dve, (f.top, g * GT + j + 1), (f.ex, g + 1))
                        dve.match_replace(d[:, j, :], top[:, j, :], d[:, j, :], 1.0).then_inc(f.rep.sem, 1)
                    wait(dve, f.rep, GT * (g + 1))
                    dve.scalar_tensor_tensor(out=kk[:, bass.ds(g * GT, GT), :], in0=d, scalar=0.5,
                                             in1=keyt[:, bass.ds(g * GT, GT)].unsqueeze(2).to_broadcast([P, GT, E]),
                                             op0=ALU.is_gt, op1=ALU.mult).then_inc(f.key.sem, 1)
                    dve.scalar_tensor_tensor(out=e_r[r], in0=d_r[r], scalar=0.5, in1=e_r[r],
                                             op0=ALU.is_gt, op1=ALU.mult).then_inc(f.es.sem, 1)
                    wait(dve, f.es, g + 1)
                    dve.tensor_reduce(den_r[r], e, X, ALU.add).then_inc(f.den.sem, 1)
                    wait(dve, f.den, g + 1)
                    dve.reciprocal(den_r[r], den_r[r]).then_inc(f.rden.sem, 1)
                    wait(dve, f.rden, g + 1)
                    wait(dve, f.ws[r], 16 * ((g - r) // 2) if isinstance(g, int) else 8 * (g - r))
                    dve.scalar_tensor_tensor(out=w_r[r].rearrange("p (j e) -> p j e", j=GT), in0=e, scalar=0.5,
                                             in1=den_r[r].unsqueeze(2).to_broadcast([P, GT, E]),
                                             op0=ALU.mult, op1=ALU.mult).then_inc(f.w.sem, 1)

                dve.wait_ge(s_cst, 7)
                route(0, 0)
                route(1, 1)
                with dve.Fori(1, NG // 2) as i:
                    for r in range(2):
                        route(2 * i + r, r)

                step = [0]

                def link(ins):
                    step[0] += 1
                    ins.then_inc(f.rnd.sem, 1)
                    wait(dve, f.rnd, step[0])

                def top_list(dst, src):
                    for c in range(0, C, 8):
                        link(dve.max(dst[:, c:c + 8], src))
                        if c + 8 < C:
                            link(dve.match_replace(src, dst[:, c:c + 8], src, 0.0))

                wait(dve, f.kts, 4)
                top_list(cand, KT)
                link(dve.tensor_copy(merged[0:E, 0:C], cand[0:E, :]))
                link(dve.tensor_copy(merged[0:E, C:2 * C], cand[E:2 * E, :]))
                top_list(slots[0:E, :], merged[0:E, :])
                wait(dve, f.slp, 1)
                both = bank[6][0:C, 0:E].rearrange("c (k two) -> c k two", two=2)
                link(dve.tensor_copy(kc[0:C, :], both[:, :, 0]))
                link(dve.tensor_copy(kc[C:P, :], both[:, :, 1]))
                link(dve.tensor_scalar(tokf, kc, -1.0, float(T), ALU.mult, ALU.add))
                link(dve.tensor_scalar(gidx, tokf, float(T - 1), None, ALU.min))
                link(dve.tensor_scalar(emp, kc, 0.0, slot_c[:, 0:1], ALU.is_equal, ALU.mult))
                link(dve.tensor_tensor(emp, emp, acc_off[:], ALU.add))
                dve.tensor_tensor(sidx, tokf, emp, ALU.add).then_inc(f.idx.sem, 1)

                def hidden(q):
                    r = q % 2
                    wait(dve, f.sil, q + 1)
                    wait(dve, f.y, q - 1)
                    dve.tensor_tensor(hid[r][0:F, :], sil[r][0:F, :], bank[2 + r][0:F, 4 * C:8 * C],
                                      ALU.mult).then_inc(f.hid.sem, 1)
                hidden(0)
                for q in range(NP2 // 2):
                    r = q % 2
                    if q + 1 < NP2 // 2:
                        hidden(q + 1)
                    wait(dve, f.y, q + 1)
                    for j in range(2):
                        k = 2 * q + j
                        wait(dve, f.sca[k % 2], 16 * ((k - NYB) // 2 + 1) if k >= NYB else 0)
                        for half in range(2):
                            rows = slice(half * C, (half + 1) * C)
                            col = D + 2 * k + half
                            dve.tensor_scalar(y_r[k % NYB][rows, :], bank[4 + r][rows, j * D:(j + 1) * D],
                                              gat[k % NGB][rows, col:col + 1], None, ALU.mult).then_inc(f.ys.sem, 1)

                def add(g, r):
                    xs = x_sb[:, bass.ds(g * GT, GT), :]
                    for a in range(NACC - 1):
                        if a == 0:
                            wait(dve, f.accl[r], 16 * NACC * ((g - r) // 2 + 1) if isinstance(g, int)
                                        else 8 * NACC * (g - r) + 16 * NACC)
                        else:
                            wait(dve, f.add, 2 * g + a)
                        if a == NACC - 2:
                            wait(dve, f.pair, g + 1)
                        src = acc_r[r * NACC + a].rearrange("p (i d) -> p i d", i=GT)
                        ins = dve.tensor_tensor(xs, xs, src, ALU.add)
                        ins.then_inc((f.add if a < NACC - 2 else f.acca).sem, 1)

                def next_stats(g):
                    wait(dve, f.acca, g + 1)
                    for j in range(GT):
                        dve.bn_stats(stats[:, bass.ds(g * GT + j, 1), :].rearrange("p a c -> p (a c)"),
                                     x_sb[:, bass.ds(g * GT + j, 1), :].rearrange("p a d -> p (a d)")).then_inc(a_stat, 1)
                if f.p == 1:
                    with dve.Fori(0, NG // 2) as i:
                        for r in range(2):
                            add(2 * i + r, r)
                    return
                for i in range(NBUF):
                    if i == 2:
                        wait(dve, f.sca[0], 16 * (NP2 // 2))
                        wait(dve, f.sca[1], 16 * (NP2 // 2))
                    ins = dve.memset(k_st[i][:, :], -1.0)
                ins.then_inc(s_kini, 1)
                dve.wait_ge(s_watt, 16 * 13)
                for i in range(2):
                    dve.tensor_copy(wqk_sb[:, i * D:(i + 1) * D].rearrange("k (d j) -> k d j", d=HD),
                                    wqk_raw[:, i * D:(i + 1) * D].rearrange("k (j d) -> k d j", d=HD)).then_inc(s_wqk, 1)
                for g in range(NG):
                    add(g, g % 2)
                    next_stats(g)
                    if g == 0:
                        variance(0, GT, a_stat, a_aggr, a_ve)
                    if g == 1:
                        inverse_std(0, GT, 1, a_sd, a_rs)
                    if g == 4:
                        dve.wait_ge(s_vini, 2)
                    if g in (4, 5, 6):
                        v_copy(g - 4, g - 4)

            def attention():
                variance(GT, NT, a_stat, a_aggr, a_ve)
                inverse_std(GT, NT, 2, a_sd, a_rs)

                def row_max(t, r, p):
                    dve.wait_ge(a_S, 8 * t + (p + 1))
                    src = psum[:, (p % 2) * 1024:(p % 2) * 1024 + 1024].rearrange("p (a k) -> p a k", a=2)
                    dve.tensor_reduce(mx_r[r % 2][:, 2 * p:2 * p + 2], src, X, ALU.max).then_inc(a_mx, 1)

                def max_high(t, r):
                    dve.wait_ge(a_mx, 8 * t + 8)
                    hl = mhl_r[r % 2].rearrange("p (g h q) -> p g h q", g=NH, h=2)
                    mx = mx_r[r % 2].rearrange("p (g q) -> p g q", g=NH)
                    dve.tensor_copy(hl[:, :, 0, :], mx).then_inc(a_hi, 1)

                def max_low(t, r):
                    dve.wait_ge(a_hi, t + 1)
                    hl = mhl_r[r % 2].rearrange("p (g h q) -> p g h q", g=NH, h=2)
                    mx = mx_r[r % 2].rearrange("p (g q) -> p g q", g=NH)
                    dve.tensor_tensor(hl[:, :, 1, :], mx, hl[:, :, 0, :], ALU.subtract).then_inc(a_hl, 1)

                def ctx_div(t, r):
                    dve.wait_ge(a_cd[r % 2], lap(t, r % 2, 2, 16 * 2))
                    dve.reciprocal(den2_r[r % 2], den2_r[r % 2]).then_inc(a_rc, 1)
                    dve.wait_ge(a_rc, t + 1)
                    wait(dve, a_use, use("o", t - 2) + 1 if not isinstance(t, int) or t >= 2 else 0)
                    dve.tensor_tensor(cT_r[r % 2], num_r[r % 2], den2_r[r % 2], ALU.mult).then_inc(a_ct, 1)

                def z_add(t):
                    dve.wait_ge(a_use, use("o", t) + 1)
                    dve.wait_ge(a_zb, t + 1)
                    z = z_sb[:, bass.ds(t * P, P)]
                    dve.tensor_tensor(z, bank[7][:, 0:P], z, ALU.add).then_inc(a_read, 1)

                def z_stats(t):
                    dve.wait_ge(a_read, use("o", t) + 1)
                    dve.bn_stats(statz[:, bass.ds(t, 1), :].rearrange("p a c -> p (a c)"),
                                 z_sb[:, bass.ds(t * P, P)]).then_inc(a_zs, 1)

                for p in range(8):
                    row_max(0, 0, p)
                max_high(0, 0)
                max_low(0, 0)
                for p in range(8):
                    row_max(1, 1, p)
                max_high(1, 1)
                max_low(1, 1)

                def step(n, r, end=NT):
                    mid = not isinstance(n, int)
                    at = lambda k: (r + k) % NBUF
                    for p in range(8):
                        if mid or n + 2 < end:
                            row_max(n + 2, at(2), p)
                        if p == 2 and (mid or n >= 2):
                            ctx_div(n - 2, at(-2))
                        if p == 4 and (mid or n + 3 < end):
                            v_copy(n + 3, at(3))
                        if p == 6 and (mid or n >= 2):
                            z_add(n - 2)
                    if mid or n + 2 < end:
                        max_high(n + 2, at(2))
                        max_low(n + 2, at(2))
                    if mid or n >= 2:
                        z_stats(n - 2)
                for n in range(NBUF):
                    step(n, n)
                with dve.Fori(1, NT // NBUF - 2) as i:
                    for r in range(NBUF):
                        step(NBUF * i + r, r)
                for n in range(NT - 2 * NBUF, NT):
                    step(n, n % NBUF)
                for t in (NT - 2, NT - 1):
                    ctx_div(t, t % NBUF)
                    z_add(t)
                    z_stats(t)
                for t in range(NT):
                    dve.wait_ge(a_zs, t + 1)
                    dve.bn_aggr(mvz[:, t, :], statz[:, t, :]).then_inc(a_za, 1)
                dve.wait_ge(a_za, NT)
                dve.tensor_scalar(rstdz[:], mvz[:, :, 1], LN_EPS, None, ALU.add).then_inc(a_zve, 1)
                dve.wait_ge(a_zsd, 1)
                dve.reciprocal(rstdz[:], rstdz[:]).then_inc(a_zrs, 1)
                dve.wait_ge(a_zrs, 1)
                dve.scalar_tensor_tensor(out=negm[:], in0=mvz[:, :, 0], scalar=-1.0, in1=rstdz[:],
                                         op0=ALU.mult, op1=ALU.mult).then_inc(a_znm, 1)
                dve.wait_ge(a_xb, NT)
                for g in range(NG):
                    z = z_sb[:, g * GT * P:(g + 1) * GT * P].rearrange("p (i d) -> p i d", i=GT)
                    xs = x_sb[:, g * GT:(g + 1) * GT, :]
                    dve.wait_ge(a_fin1, g + 1)
                    dve.tensor_tensor(xs, xs, z, ALU.add).then_inc(a_fin, 1)
                    dve.wait_ge(a_fin, g + 1)
                    for t in range(g * GT, (g + 1) * GT):
                        dve.bn_stats(stats[:, t, :], x_sb[:, t, :]).then_inc(ffns[1].stat.sem, 1)

            for i in range(NT):
                if i % (NT // 4) == 0:
                    dve.wait_ge(s_x[i // (NT // 4)], 16)
                dve.bn_stats(stats[:, i, :], x_sb[:, i, :]).then_inc(ffns[0].stat.sem, 1)
            dve.wait_ge(s_rwp, 1)
            dve.tensor_copy(rwT[:], bank[0][:, 0:E]).then_inc(s_rws, 1)
            ffn(ffns[0])
            attention()
            ffn(ffns[1])

        @block.scalar
        def _(act):
            def ffn(f):
                wait(act, f.ve, 1)
                act.activation(rstd[:], rstd[:], ACT.Sqrt).then_inc(f.sd.sem, 1)

                def route(g, r):
                    wait(act, f.xtp, g + 1)
                    wait(act, f.lg, g - 1)
                    act.activation(xT_r[r], bank[r][:], ACT.Copy).then_inc(f.xts.sem, 1)
                    act.activation(xT_all[:, bass.ds(g * (GT * P), GT * P)], bank[r][:], ACT.Copy).then_inc(f.xts.sem, 1)
                    wait(act, f.d, GT * (g + 1))
                    wait(act, f.w, g - 1)
                    act.activation(e_r[r], d_r[r], ACT.Exp).then_inc(f.ex.sem, 1)
                route(0, 0)
                route(1, 1)
                with act.Fori(1, NG // 2) as i:
                    for r in range(2):
                        route(2 * i + r, r)
                for b in range(4):
                    wait(act, f.ktp, b + 1)
                    act.activation(KT[:, b * 512:(b + 1) * 512], bank[4 + b][:], ACT.Copy).then_inc(f.kts.sem, 1)

                def shared_up(g, r):
                    wait(act, f.shp, g + 1)
                    wait(act, f.shh, g - 1)
                    act.activation(shs[r][0:F, :], bank[r][0:F, :], ACT.Silu).then_inc(f.shs.sem, 1)
                    act.activation(shu[r][0:F, :], bank[2 + r][0:F, :], ACT.Copy).then_inc(f.shc.sem, 1)

                def shared_out(g, r):
                    wait(act, f.sho, g + 1)
                    wait(act, f.shx, g - 1)
                    act.activation(shy[r], bank[4 + r][:], ACT.Copy, scale=0.5).then_inc(f.shy.sem, 1)
                shared_up(0, 0)
                shared_up(1, 1)
                shared_out(0, 0)
                with act.Fori(1, NG // 2) as i:
                    for r in range(2):
                        shared_up(2 * i + r, r)
                        shared_out(2 * i + (r - 1), 1 - r)
                shared_out(NG - 1, 1)

                for q in range(NP2 // 2):
                    r = q % 2
                    wait(act, f.gtp, q + 1)
                    wait(act, f.gu, q - 1)
                    act.activation(gT[r], bank[r][:, 0:2 * P], ACT.Copy).then_inc(f.gts.sem, 1)
                    wait(act, f.gu, q + 1)
                    wait(act, f.hid, q - 1)
                    act.activation(sil[r][0:F, :], bank[2 + r][0:F, 0:4 * C], ACT.Silu).then_inc(f.sil.sem, 1)

            def attention():
                def std(first, last, count):
                    act.wait_ge(a_ve, count)
                    act.activation(rstd[:, first:last], rstd[:, first:last], ACT.Sqrt).then_inc(a_sd, 1)
                std(0, GT, 1)

                def xT_copy(t, r):
                    act.wait_ge(a_use, use("x", t) + 1)
                    act.activation(xTt_r[r % 2], bank[7][:, 0:P], ACT.Copy).then_inc(a_read, 1)

                def qk_copy(t, r):
                    act.wait_ge(a_use, use("q", t) + 1)
                    wait(act, a_parts, t - 1)
                    for i in range(2):
                        ins = act.activation(qk_r[r % 2][:, i * P:(i + 1) * P].rearrange("p (s g) -> p g s", g=NH),
                                             bank[7][:, i * P:(i + 1) * P].rearrange("p (g s) -> p g s", g=NH),
                                             ACT.Identity, bias=bqk_sb[:, i:i + 1])
                    ins.then_inc(a_read, 1)

                def max_copy(t, r):
                    act.wait_ge(a_use, use("m", t) + 1)
                    if not isinstance(t, int) or t >= 2:
                        act.wait_ge(a_mrow[(r - 2) % NBUF], lap(t - 2, (r - 2) % NBUF, NBUF, 16))
                    act.activation(mT_r[r % 2].rearrange("m (c g) -> m g c", g=NH),
                                   bank[7][0:8, 0:2 * P].bitcast(BF16).rearrange("m (g c) -> m g c", g=NH),
                                   ACT.Copy).then_inc(a_read, 1)

                def ctx_copy(t, r):
                    act.wait_ge(a_PV, 4 * t + 4)
                    if not isinstance(t, int) or t >= 2:
                        act.wait_ge(a_cd[r % 2], lap(t - 2, r % 2, 2, 16 * 2))
                    act.activation(ctx_r[r % 2], bank[6][:, :], ACT.Copy).then_inc(a_cx, 1)

                def step(n, r, end=NT):
                    mid = not isinstance(n, int)
                    for tau in range(16):
                        kt, g = tau // 4, tau % 4
                        act.wait_ge(a_ST, 16 * n + (tau + 1))
                        if g == 0:
                            wait(act, a_PV, 4 * n + (kt - 1))
                        act.activation(p_r[tau % NPB], bank[4 + tau % 2][:, :], ACT.Exp, scale=SCALE).then_inc(a_P, 1)
                        if tau == 0 and (mid or n + 4 < end):
                            xT_copy(n + 4, r)
                        if tau == 3 and (mid or n + 1 < end):
                            max_copy(n + 1, (r + 1) % NBUF)
                        if tau == 5 and (mid or n >= 1):
                            ctx_copy(n - 1, (r - 1) % NBUF)
                        if tau == 7 and (mid or n + 4 < end):
                            qk_copy(n + 4, r)
                for t in range(NBUF):
                    if t == 3:
                        std(GT, NT, 2)
                    xT_copy(t, t)
                    qk_copy(t, t)
                max_copy(0, 0)
                for n in range(NBUF):
                    step(n, n)
                with act.Fori(1, NT // NBUF - 1) as i:
                    for r in range(NBUF):
                        step(NBUF * i + r, r)
                for n in range(NT - NBUF, NT):
                    step(n, n % NBUF)
                ctx_copy(NT - 1, (NT - 1) % NBUF)
                act.wait_ge(a_zve, 1)
                act.activation(rstdz[:], rstdz[:], ACT.Sqrt).then_inc(a_zsd, 1)
                act.wait_ge(a_znm, 1)
                for t in range(NT):
                    z = z_sb[:, t * P:(t + 1) * P]
                    act.activation(z, z, ACT.Identity, scale=rstdz[:, t:t + 1], bias=negm[:, t:t + 1]).then_inc(a_zn, 1)

            ffn(ffns[0])
            attention()
            ffn(ffns[1])

        @block.tensor
        def _(pe):
            def ffn(f):
                def route(g, r):
                    wait(pe, f.xn, g + 1)
                    wait(pe, f.xts, 2 * (g - 1))
                    for j in range(GT):
                        ins = pe.transpose(bank[r][:, j * P:(j + 1) * P], xn_sb[:, r, j, :], ident[:])
                    ins.then_inc(f.xtp.sem, 1)
                    wait(pe, f.xts, 2 * g + 1)
                    wait(pe, f.d, GT * (g - 1))
                    for j in range(GT):
                        ins = pe.matmul(bank[2 + r][:, j * E:(j + 1) * E], xT_r[r][:, j * P:(j + 1) * P], rwT[:],
                                        start=True, stop=True)
                    ins.then_inc(f.lg.sem, 1)
                route(0, 0)
                route(1, 1)
                with pe.Fori(1, NG // 2) as i:
                    for r in range(2):
                        route(2 * i + r, r)

                for u in range(NT // 2):
                    if u % 4 == 0:
                        wait(pe, f.key, (2 * u + 8) // GT)
                    ins = pe.transpose(bank[4 + u // 4][:, (u % 4) * P:(u % 4 + 1) * P], key[:, u * P:(u + 1) * P], ident[:])
                    if u % 4 == 3:
                        ins.then_inc(f.ktp.sem, 1)
                pe.wait_ge(s_wsh, 32)

                def up(g, r):
                    wait(pe, f.shc, g - 1)
                    pe.matmul(bank[r][0:F, :], wsgu_sb[:, 0:F], xT_all[:, bass.ds(g * (GT * P), GT * P)],
                              start=True, stop=True)
                    pe.matmul(bank[2 + r][0:F, :], wsgu_sb[:, F:2 * F], xT_all[:, bass.ds(g * (GT * P), GT * P)],
                              start=True, stop=True).then_inc(f.shp.sem, 1)

                def down(g, r):
                    wait(pe, f.shh, g + 1)
                    wait(pe, f.shy, g - 1)
                    for j in range(GT):
                        ins = pe.matmul(bank[4 + r][:, j * D:(j + 1) * D], shh[r][0:F, j * P:(j + 1) * P], wsd_sb[:],
                                        start=True, stop=True)
                    ins.then_inc(f.sho.sem, 1)

                wait(pe, f.xts, 2 * NG)
                wait(pe, f.kts, 4)
                up(0, 0)
                up(1, 1)
                down(0, 0)
                with pe.Fori(1, NG // 2) as i:
                    up(2 * i, 0)
                    down(2 * i - 1, 1)
                    up(2 * i + 1, 1)
                    down(2 * i, 0)
                down(NG - 1, 1)
                wait(pe, f.rnd, 32)
                pe.transpose(bank[6][0:C, 0:E], slots[0:E, :], ident[0:E, 0:E]).then_inc(f.slp.sem, 1)

                pe.wait_ge(s_wexp, 48)

                def slots_t(q):
                    r = q % 2
                    wait(pe, f.gts, q - 1)
                    for j in range(2):
                        k = 2 * q + j
                        wait(pe, f.gat[k % NGB], 16 * (k // NGB + 1))
                        ins = pe.transpose(bank[r][:, j * P:(j + 1) * P], gat[k % NGB][:, 0:D], ident[:])
                    ins.then_inc(f.gtp.sem, 1)

                def down_e(q):
                    r = q % 2
                    wait(pe, f.hid, q + 1)
                    wait(pe, f.ys, 4 * (q - 1))
                    for j in range(2):
                        for half in range(2):
                            e = 4 * q + 2 * j + half
                            rows = slice(half * C, (half + 1) * C)
                            ins = pe.matmul(bank[4 + r][rows, j * D:(j + 1) * D],
                                            hid[r][0:F, (2 * j + half) * C:(2 * j + half + 1) * C], wd_sb[:, e, :],
                                            start=True, stop=True)
                    ins.then_inc(f.y.sem, 1)

                wait(pe, f.shc, NG)
                wait(pe, f.shy, NG)
                slots_t(0)
                for q in range(NP2 // 2):
                    r = q % 2
                    wait(pe, f.gts, q + 1)
                    wait(pe, f.hid, q - 1)
                    for w, off in ((wg_sb, 0), (wu_sb, 4 * C)):
                        for m in range(4):
                            ins = pe.matmul(bank[2 + r][0:F, off + m * C:off + (m + 1) * C], w[:, 4 * q + m, :],
                                            gT[r][:, m * C:(m + 1) * C], start=True, stop=True)
                    ins.then_inc(f.gu.sem, 1)
                    if q + 1 < NP2 // 2:
                        slots_t(q + 1)
                    if q:
                        down_e(q - 1)
                down_e(NP2 // 2 - 1)

            pe.wait_ge(s_cst, 2)
            pe.wait_ge(s_wr, 16)
            pe.transpose(bank[0][:, 0:E], rw_sb[:], ident[0:E, 0:E]).then_inc(s_rwp, 1)
            pe.wait_ge(s_rws, 1)
            def attention():
                def misc(kind, t):
                    i = use(kind, t)
                    wait(pe, a_read, i)

                def xT(t, r):
                    pe.wait_ge(a_xn, t + 1)
                    misc("x", t)
                    pe.transpose(bank[7][:, 0:P], xn_r[r % 2], ident[:]).then_inc(a_use, 1)

                def qk(t, r):
                    misc("q", t)
                    for i in range(2):
                        ins = pe.matmul(bank[7][:, i * P:(i + 1) * P], wqk_sb[:, i * D:(i + 1) * D], xTt_r[r % 2],
                                        start=True, stop=True)
                    ins.then_inc(a_use, 1)

                def v(t, r):
                    misc("v", t)
                    for g in range(NH):
                        for jj in range(4):
                            ins = pe.matmul(bank[7][jj * 32:(jj + 1) * 32, g * 32:(g + 1) * 32],
                                            xTt_r[r % 2][:, g * HS:(g + 1) * HS],
                                            wv_sb[:].rearrange("e (k jj d) -> e jj k d", k=4, jj=4)[:, jj, :, :],
                                            start=True, stop=True, tile_position=(0, jj * 32))
                    ins.then_inc(a_use, 1)

                def maxT(t, r):
                    pe.wait_ge(a_hl, t + 1)
                    misc("m", t)
                    for g in range(NH):
                        ins = pe.transpose(bank[7][0:8, g * P // 2:(g + 1) * P // 2].bitcast(BF16),
                                           mhl_r[r % 2][:, 8 * g:8 * g + 8], identb[:])
                    ins.then_inc(a_use, 1)

                def proj(t, r):
                    pe.wait_ge(a_ct, t + 1)
                    misc("o", t)
                    pe.matmul(bank[7][:, 0:D], cT_r[r % 2], wo_sb[:], start=True, stop=True).then_inc(a_use, 1)

                def scores(t, r, tau):
                    g, qt = tau // 4, tau % 4
                    if tau == 0:
                        pe.wait_ge(a_stk[r], lap(t, r, NBUF, 16 * (NPART + 1)))
                    if tau % 2 == 0:
                        wait(pe, a_mx, 8 * t + (tau // 2 - 1))
                    rows = slice(0, MR)
                    ins = pe.matmul(bank[tau % 4][:, :], heads(q_st[r], rows, g)[:, qt * P:(qt + 1) * P],
                                    heads(k_st[r], rows, g), start=True, stop=True)
                    if tau % 2:
                        ins.then_inc(a_S, 1)

                def scores_t(t, r, tau):
                    kt, g = tau // 4, tau % 4
                    if tau == 0:
                        pe.wait_ge(a_mrow[r], lap(t, r, NBUF, 16))
                    wait(pe, a_P, 16 * t + (tau - 1))
                    rows = slice(0, P)
                    keys = heads(k_st[r], rows, g)[:, kt * P:(kt + 1) * P]
                    pe.matmul(bank[4 + tau % 2][:, :], keys, heads(q_st[r], rows, g), start=True, stop=True)\
                      .then_inc(a_ST, 1)

                def pv(t, r, kt):
                    pe.wait_ge(a_P, 16 * t + (4 * kt + 4))
                    if kt == 0:
                        wait(pe, a_cx, t)
                        pe.wait_ge(a_read, use("v", t) + 1)
                    for g in range(NH):
                        ins = pe.matmul(bank[6][32 * g:32 * g + 32, :], v_r[r][:, g, kt, :], p_r[(4 * kt + g) % NPB],
                                        start=(kt == 0), stop=(kt == 3), tile_position=(0, 32 * g))
                    ins.then_inc(a_PV, 1)

                def step(n, r, end=NT):
                    mid = not isinstance(n, int)
                    at = lambda k: (r + k) % NBUF
                    for tau in range(16):
                        if tau == 0 and (mid or n + 4 < end):
                            xT(n + 4, r)
                        if tau == 3 and (mid or n + 1 < end):
                            maxT(n + 1, at(1))
                        if tau == 6 and (mid or n + 4 < end):
                            qk(n + 4, r)
                        if tau == 10 and (mid or n + 3 < end):
                            v(n + 3, at(3))
                        if tau == 14 and (mid or n >= 2):
                            proj(n - 2, at(-2))
                        scores_t(n, r, tau)
                        if mid or n + 2 < end:
                            scores(n + 2, at(2), tau)
                        if tau == 3 and (mid or n >= 1):
                            pv(n - 1, at(-1), 3)
                        if tau % 4 == 3 and tau > 3:
                            pv(n, r, tau // 4 - 1)

                pe.wait_ge(s_wqk, 2)
                wait(pe, ffns[0].ys, 2 * NP2)

                def prep(t):
                    xT(t, t)
                    qk(t, t)
                    if t < 3:
                        v(t, t)
                for t in range(3):
                    prep(t)
                for tau in range(16):
                    scores(0, 0, tau)
                prep(3)
                for tau in range(16):
                    scores(1, 1, tau)
                    if tau == 1:
                        maxT(0, 0)
                for n in range(NBUF):
                    step(n, n)
                with pe.Fori(1, NT // NBUF - 1) as i:
                    for r in range(NBUF):
                        step(NBUF * i + r, r)
                for n in range(NT - NBUF, NT):
                    step(n, n % NBUF)
                pv(NT - 1, (NT - 1) % NBUF, 3)
                for t in (NT - 2, NT - 1):
                    proj(t, t % NBUF)

            ffn(ffns[0])
            attention()
            ffn(ffns[1])



_INS = ["L0_attn_x", "L0_attn_wq", "L0_attn_bq", "L0_attn_wk", "L0_attn_bk", "L0_attn_wv", "L0_attn_bv", "L0_attn_wo",
        "L0_attn_bo", "L0_attn_gamma", "L0_attn_beta", "L0_ffn_router_w", "L0_ffn_w_gate", "L0_ffn_w_up",
        "L0_ffn_w_down", "L0_ffn_ws_gate_up", "L0_ffn_ws_down"]


def kernel(**inputs):
    import numpy as np
    import concourse.bacc as bacc
    from concourse.bass_utils import run_bass_kernel_spmd

    nc = bacc.Bacc("TRN2", target_bir_lowering=False, num_devices=1)
    arrays, args = {}, []
    for name in _INS:
        a = np.ascontiguousarray(inputs[name])
        arrays[f"in_{name}"] = a
        args.append(nc.dram_tensor(f"in_{name}", a.shape, mybir.dt.from_np(a.dtype), kind="ExternalInput").ap())
    out = nc.dram_tensor("out_x", inputs["L0_attn_x"].shape, F32, kind="ExternalOutput").ap()
    macaron_kernel(nc, *args, out)
    r = run_bass_kernel_spmd(nc, [arrays], core_ids=[0])
    return r.results[0]["out_x"]
```
